# Optimizing a Trainium2 kernel written in Bass

```python
import numpy as np
import jax
import jax.numpy as jnp

def _softmax(x, axis=-1):
    return jax.nn.softmax(x, axis=axis)

def _gelu(x):
    return jax.nn.gelu(x, approximate=True)

def _silu(x):
    return jax.nn.silu(x)

def _sigmoid(x):
    return jax.nn.sigmoid(x)

def _layernorm(x, axis=-1, eps=1e-05):
    m = jnp.mean(x, axis=axis, keepdims=True)
    v = jnp.var(x, axis=axis, keepdims=True)
    return (x - m) / jnp.sqrt(v + eps)

def _scatter_add(tgt, idx, src, axis=0):
    return tgt.at[idx].add(src)

def _segment_sum(src, seg, n):
    return jax.ops.segment_sum(src, seg, n)
kernel_name = 'mk_decoder_preln_d1_seqx_r8_e73cdf'

def setup_inputs(seed: int=0):
    np.random.seed(seed)
    _w = jnp.asarray

    def _rec_inputs():
        import jax
        import jax.numpy as jnp
        _rk = jax.random.key(seed)
        x = -0.0002928 + 1 * jax.random.normal(jax.random.fold_in(_rk, 1), (16, 128, 256), jnp.float32)
        _lenS = 128 - jax.random.randint(jax.random.fold_in(_rk, 7), (16,), 0, max(1, 128 // 4) + 1, jnp.int32)
        _lenS2 = 128 - jax.random.randint(jax.random.fold_in(_rk, 8), (16,), 0, max(1, 128 // 4) + 1, jnp.int32)
        _ctx_2048P = jax.random.normal(jax.random.fold_in(_rk, 11), (16, 16, 256), jnp.float32)
        _ctx_2048c = jax.random.dirichlet(jax.random.fold_in(_rk, 511), 0.3 * jnp.ones((16,), jnp.float32), (16, 128))
        _ctx_2048t = jnp.einsum('bsk,bkd->bsd', _ctx_2048c, _ctx_2048P)
        _ctx_2048t = _ctx_2048t * jax.lax.rsqrt(jnp.mean(jnp.square(_ctx_2048t)) + 1e-12) * 0.953939
        ctx_2048 = -1.39393e-06 + 0.999914 * (_ctx_2048t + 0.3 * jax.random.normal(jax.random.fold_in(_rk, 611), (16, 128, 256), jnp.float32))
        _validS = jnp.arange(128)[None, :] < _lenS[:, None]
        _validS2 = jnp.arange(128)[None, :] < _lenS2[:, None]
        _causal = jnp.tril(jnp.ones((128, 128), dtype=bool))
        mask_BxS2_if1 = jnp.where(jnp.ones((16, 128), dtype=bool), 1, 0).astype(jnp.int32)
        return (x, ctx_2048, mask_BxS2_if1)
    x, ctx_2048, mask_BxS2_if1 = _rec_inputs()

    def _L0_attn_setup():
        import jax, jax.numpy as jnp
        import numpy as np
        B, T, D_MODEL = (4, 512, 256)
        D_LATENT = 64
        D_COMP = 32
        THETA = 10000.0
        LN_EPS = 1e-05

        def _rope_tables(seq_len: int, dim: int):
            inv_freq = 1.0 / THETA ** (jnp.arange(0, dim, 2, dtype=jnp.float32) / dim)
            freqs = jnp.arange(seq_len, dtype=jnp.float32)[:, None] * inv_freq[None, :]
            cos = jnp.concatenate([jnp.cos(freqs), jnp.cos(freqs)], axis=-1)
            sin = jnp.concatenate([jnp.sin(freqs), jnp.sin(freqs)], axis=-1)
            return (cos, sin)

        def _rotate_half(x):
            x1, x2 = jnp.split(x, 2, axis=-1)
            return jnp.concatenate([-x2, x1], axis=-1)
        key = jax.random.key(seed)
        ks = jax.random.split(key, 8)
        s = 0.02
        return {'x': jax.random.normal(ks[0], (B, T, D_MODEL), dtype=jnp.float32), 'W_to_kv': jax.random.normal(ks[1], (D_LATENT, D_MODEL), dtype=jnp.float32) * s, 'W_compress': jax.random.normal(ks[2], (D_COMP, D_LATENT), dtype=jnp.float32) * s, 'ln_gamma': jnp.ones((D_COMP,), dtype=jnp.float32), 'ln_beta': jnp.zeros((D_COMP,), dtype=jnp.float32), 'W_q_comp': jax.random.normal(ks[3], (D_COMP, D_COMP), dtype=jnp.float32) * s, 'W_kv_comp': jax.random.normal(ks[4], (2 * D_COMP, D_COMP), dtype=jnp.float32) * s, 'W_comp2lat': jax.random.normal(ks[5], (D_LATENT, D_COMP), dtype=jnp.float32) * s, 'W_out_res': jnp.zeros((D_MODEL, D_LATENT), dtype=jnp.float32), 'b_out_res': jnp.zeros((D_MODEL,), dtype=jnp.float32)}
    _L0_attn_all = _L0_attn_setup()
    _L0_attn_in = {k: v for k, v in _L0_attn_all.items() if k in ('W_to_kv', 'W_compress', 'ln_gamma', 'ln_beta', 'W_q_comp', 'W_kv_comp', 'W_comp2lat', 'W_out_res', 'b_out_res')}
    del _L0_attn_all

    def _L0_xattn_setup():
        import jax, jax.numpy as jnp
        import numpy as np
        D_MODEL = 256
        N_HEADS = 32
        N_GROUPS = 8
        HEAD_DIM = D_MODEL // N_HEADS
        BATCH, SEQ = (2, 128)
        NEG_INF = float('-inf')
        key = jax.random.key(seed)
        ks = jax.random.split(key, 9)
        s = 0.02
        return {'Q': jax.random.normal(ks[0], (BATCH, SEQ, D_MODEL), jnp.float32), 'K': jax.random.normal(ks[1], (BATCH, SEQ, D_MODEL), jnp.float32), 'V': jax.random.normal(ks[2], (BATCH, SEQ, D_MODEL), jnp.float32), 'attention_mask': jnp.ones((BATCH, SEQ), jnp.int32), 'w_q': jax.random.normal(ks[3], (D_MODEL, D_MODEL), jnp.float32) * s, 'w_k': jax.random.normal(ks[4], (HEAD_DIM * N_GROUPS, D_MODEL), jnp.float32) * s, 'w_v': jax.random.normal(ks[5], (HEAD_DIM * N_GROUPS, D_MODEL), jnp.float32) * s, 'w_o': jax.random.normal(ks[6], (D_MODEL, D_MODEL), jnp.float32) * s, 'b_o': jnp.zeros((D_MODEL,), jnp.float32)}
    _L0_xattn_all = _L0_xattn_setup()
    _L0_xattn_in = {k: v for k, v in _L0_xattn_all.items() if k in ('w_q', 'w_k', 'w_v', 'w_o', 'b_o')}
    del _L0_xattn_all

    def _L0_ffn_setup():
        import jax, jax.numpy as jnp
        import numpy as np
        NUM_EXPERTS = 32
        TOP_K = 8
        THRESHOLD = 0.8
        HIDDEN = 256
        INTER = 96
        key = jax.random.key(seed)
        k1, k2, k3, k4 = jax.random.split(key, 4)
        hidden_states = jax.random.normal(k1, (2, 128, HIDDEN), jnp.float32)
        gate_weight = jax.random.normal(k2, (NUM_EXPERTS, HIDDEN), jnp.float32) * 0.02
        gate_up_proj = jax.random.normal(k3, (NUM_EXPERTS, 2 * INTER, HIDDEN), jnp.float32) * 0.02
        down_proj = jax.random.normal(k4, (NUM_EXPERTS, HIDDEN, INTER), jnp.float32) * 0.02
        return {'hidden_states': hidden_states, 'gate_weight': gate_weight, 'gate_up_proj': gate_up_proj, 'down_proj': down_proj}
    _L0_ffn_all = _L0_ffn_setup()
    _L0_ffn_in = {k: v for k, v in _L0_ffn_all.items() if k in ('gate_weight', 'gate_up_proj', 'down_proj')}
    del _L0_ffn_all
    return {'x': x, 'ctx_2048': ctx_2048, 'mask_BxS2_if1': mask_BxS2_if1, 'L0_attn_W_to_kv': _L0_attn_in['W_to_kv'], 'L0_attn_W_compress': _L0_attn_in['W_compress'], 'L0_attn_ln_gamma': _L0_attn_in['ln_gamma'], 'L0_attn_ln_beta': _L0_attn_in['ln_beta'], 'L0_attn_W_q_comp': _L0_attn_in['W_q_comp'], 'L0_attn_W_kv_comp': _L0_attn_in['W_kv_comp'], 'L0_attn_W_comp2lat': _L0_attn_in['W_comp2lat'], 'L0_attn_W_out_res': _L0_attn_in['W_out_res'], 'L0_attn_b_out_res': _L0_attn_in['b_out_res'], 'L0_xattn_w_q': _L0_xattn_in['w_q'], 'L0_xattn_w_k': _L0_xattn_in['w_k'], 'L0_xattn_w_v': _L0_xattn_in['w_v'], 'L0_xattn_w_o': _L0_xattn_in['w_o'], 'L0_xattn_b_o': _L0_xattn_in['b_o'], 'L0_ffn_gate_weight': _L0_ffn_in['gate_weight'], 'L0_ffn_gate_up_proj': _L0_ffn_in['gate_up_proj'], 'L0_ffn_down_proj': _L0_ffn_in['down_proj']}

def reference(x, ctx_2048, mask_BxS2_if1, L0_attn_W_to_kv, L0_attn_W_compress, L0_attn_ln_gamma, L0_attn_ln_beta, L0_attn_W_q_comp, L0_attn_W_kv_comp, L0_attn_W_comp2lat, L0_attn_W_out_res, L0_attn_b_out_res, L0_xattn_w_q, L0_xattn_w_k, L0_xattn_w_v, L0_xattn_w_o, L0_xattn_b_o, L0_ffn_gate_weight, L0_ffn_gate_up_proj, L0_ffn_down_proj):
    import jax
    import jax.numpy as jnp

    def _L0_attn_ref(x, W_to_kv, W_compress, ln_gamma, ln_beta, W_q_comp, W_kv_comp, W_comp2lat, W_out_res, b_out_res):
        import jax, jax.numpy as jnp
        import numpy as np
        B, T, D_MODEL = (4, 512, 256)
        D_LATENT = 64
        D_COMP = 32
        THETA = 10000.0
        LN_EPS = 1e-05

        def _rope_tables(seq_len: int, dim: int):
            inv_freq = 1.0 / THETA ** (jnp.arange(0, dim, 2, dtype=jnp.float32) / dim)
            freqs = jnp.arange(seq_len, dtype=jnp.float32)[:, None] * inv_freq[None, :]
            cos = jnp.concatenate([jnp.cos(freqs), jnp.cos(freqs)], axis=-1)
            sin = jnp.concatenate([jnp.sin(freqs), jnp.sin(freqs)], axis=-1)
            return (cos, sin)

        def _rotate_half(x):
            x1, x2 = jnp.split(x, 2, axis=-1)
            return jnp.concatenate([-x2, x1], axis=-1)
        Bx, Tx, _ = x.shape
        dc = W_compress.shape[0]
        kv_latent = x @ W_to_kv.T
        c = kv_latent @ W_compress.T
        mu = jnp.mean(c, axis=-1, keepdims=True)
        var = jnp.mean((c - mu) ** 2, axis=-1, keepdims=True)
        ch = (c - mu) * jax.lax.rsqrt(var + LN_EPS) * ln_gamma + ln_beta
        q = ch @ W_q_comp.T
        kv = ch @ W_kv_comp.T
        k, v = jnp.split(kv, 2, axis=-1)
        cos, sin = _rope_tables(Tx, dc)
        q = q * cos + _rotate_half(q) * sin
        k = k * cos + _rotate_half(k) * sin
        scale = 1.0 / jnp.sqrt(jnp.float32(dc))
        scores = jnp.einsum('btd,bsd->bts', q, k) * scale
        causal = jnp.tril(jnp.ones((Tx, Tx), dtype=bool))
        scores = jnp.where(causal[None], scores, jnp.float32(-1e+30))
        attn = jax.nn.softmax(scores, axis=-1)
        o = jnp.einsum('bts,bsd->btd', attn, v)
        z = o @ W_comp2lat.T
        out = z @ W_to_kv + z @ W_out_res.T + b_out_res
        return out

    def _L0_xattn_ref(Q, K, V, attention_mask, w_q, w_k, w_v, w_o, b_o):
        import jax, jax.numpy as jnp
        import numpy as np
        D_MODEL = 256
        N_HEADS = 32
        N_GROUPS = 8
        HEAD_DIM = D_MODEL // N_HEADS
        BATCH, SEQ = (2, 128)
        NEG_INF = float('-inf')
        B, S, D = Q.shape
        G, HG, HD = (N_GROUPS, N_HEADS // N_GROUPS, HEAD_DIM)
        q = (Q @ w_q.T).reshape(B, S, G, HG, HD)
        k = (K @ w_k.T).reshape(B, S, G, HD)
        v = (V @ w_v.T).reshape(B, S, G, HD)
        scale = jnp.sqrt(jnp.float32(HD))
        scores = jnp.einsum('bnghd,bmgd->bnghm', q, k) / scale
        pad = (attention_mask == 0)[:, None, None, None, :]
        scores = jnp.where(pad, NEG_INF, scores)
        causal = jnp.tril(jnp.ones((S, S), bool))[None, :, None, None, :]
        scores = jnp.where(causal, scores, NEG_INF)
        attn = jax.nn.softmax(scores, axis=-1)
        out = jnp.einsum('bnghm,bmgd->bnghd', attn, v).reshape(B, S, D)
        return out @ w_o.T + b_o

    def _L0_ffn_ref(hidden_states, gate_weight, gate_up_proj, down_proj):
        import jax, jax.numpy as jnp
        import numpy as np
        NUM_EXPERTS = 32
        TOP_K = 8
        THRESHOLD = 0.8
        HIDDEN = 256
        INTER = 96
        B, S, H = hidden_states.shape
        x = hidden_states.reshape(-1, H)
        logits = x @ gate_weight.T
        probs = jax.nn.softmax(logits.astype(jnp.float32), axis=-1).astype(logits.dtype)
        top_vals, top_idx = jax.lax.top_k(probs, TOP_K)
        renorm = top_vals / jnp.clip(jnp.sum(top_vals, axis=-1, keepdims=True), 1e-12)
        cum = jnp.cumsum(renorm, axis=-1)
        num_keep = jnp.minimum(jnp.sum((cum < THRESHOLD).astype(jnp.int32), axis=-1) + 1, TOP_K)
        active = jnp.arange(TOP_K)[None, :] < num_keep[:, None]
        rw = top_vals * active.astype(top_vals.dtype)
        rw = rw / jnp.clip(jnp.sum(rw, axis=-1, keepdims=True), 1e-12)
        combine = jnp.sum(jax.nn.one_hot(top_idx, NUM_EXPERTS, dtype=rw.dtype) * rw[..., None], axis=1)

        def body(acc, params):
            w_gu, w_d, ce = params
            gu = x @ w_gu.T
            g, u = jnp.split(gu, 2, axis=-1)
            h = jax.nn.silu(g) * u
            return (acc + h @ w_d.T * ce[:, None], None)
        out, _ = jax.lax.scan(body, jnp.zeros_like(x), (gate_up_proj, down_proj, combine.T))
        return out.reshape(B, S, H)
    x = x + _L0_attn_ref(_layernorm(x, axis=-1), L0_attn_W_to_kv, L0_attn_W_compress, L0_attn_ln_gamma, L0_attn_ln_beta, L0_attn_W_q_comp, L0_attn_W_kv_comp, L0_attn_W_comp2lat, L0_attn_W_out_res, L0_attn_b_out_res)
    x = x + _L0_xattn_ref(_layernorm(x, axis=-1), ctx_2048, ctx_2048, mask_BxS2_if1, L0_xattn_w_q, L0_xattn_w_k, L0_xattn_w_v, L0_xattn_w_o, L0_xattn_b_o)
    x = x + _L0_ffn_ref(_layernorm(x, axis=-1), L0_ffn_gate_weight, L0_ffn_gate_up_proj, L0_ffn_down_proj)
    return x

_drawn_inputs = setup_inputs


def setup_inputs(seed=0):
    import zlib

    import numpy as np

    out = dict(_drawn_inputs(seed))
    spreads = {'L0_attn_ln_gamma': (1.0, 0.6),
     'L0_attn_ln_beta': (0.0, 0.8),
     'L0_attn_W_out_res': (0.0, 0.8),
     'L0_attn_b_out_res': (0.0, 0.1),
     'L0_xattn_b_o': (0.0, 0.1)}
    factors = {'L0_attn_W_to_kv': 8.0,
     'L0_attn_W_compress': 8.0,
     'L0_attn_W_q_comp': 8.0,
     'L0_attn_W_kv_comp': 8.0,
     'L0_attn_W_comp2lat': 8.0,
     'L0_xattn_w_q': 8.0,
     'L0_xattn_w_k': 8.0,
     'L0_ffn_gate_weight': 8.0,
     'L0_ffn_gate_up_proj': 8.0,
     'L0_ffn_down_proj': 8.0}
    for name, (base, spread) in spreads.items():
        noise = np.random.default_rng([zlib.crc32(name.encode()), seed]).standard_normal(out[name].shape)
        drawn = base * np.exp(spread * noise) if base else spread * noise
        out[name] = jnp.asarray(drawn.astype(out[name].dtype))
    for name, factor in factors.items():
        out[name] = (out[name] * factor).astype(out[name].dtype)
    return out
```

```python
import concourse.bass as bass
from concourse import mybir
from contextlib import ExitStack

NB, P, D = 16, 128, 256
KC = D // P
NE, NI = 32, 96
NJ, EJ = 8, 4
BW = EJ * NI
PW = 2 * BW
TC = BW // P
NG, HG, HD = 8, 4, 8
GD = NG * HD
DL, DC = 64, 32
CW = 2 * P + 4 * DC + NG + HG + NG
BIG = 1e30
EPS = 1e-5
NPT = 4
KEEP = 0.8


def front_steps():
    return [f"r{n}" for n in range(1, 20)]


def cross_steps():
    scores = [f"s{g}" for g in range(NPT)]
    for g in range(NG):
        scores += [f"pv{g}"] + ([f"s{g + NPT}"] if g + NPT < NG else [])
    return [f"mx{u}" for u in range(8)] + ["c"] + scores + ["on", "oT", "wo", "n3"]


ORDER = """
xT mx0 mx1 mx2 lg gate1 gu0 mx3 mx4 gate2 ab0 r1
gu1 mx5 r2 T0 mx6 ab1 r3 mx7 D0
gu2 r4 c T1 ab2 r5 s0 s1 D1 r6
gu3 s2 r7 T2 s3 ab3 r8 D2 pv0
gu4 s4 r9 pv1 T3 s5 ab4 r10 pv2 D3 s6 r11
gu5 pv3 s7 r12 T4 pv4 ab5 r13 D4 pv5
gu6 r14 pv6 T5 pv7 ab6 r15 D5 on oT
gu7 r16 T6 wo ab7 r17 D6 n3 r18
T7 r19 D7 y
""".split()


def decoder_kernel(nc, x, ctxT, mask, wgu, wd, gateT, wtokv, wcompT, woutresT, wc2l, wqkv, gb, bias2,
                   wq, wkv, wo, consts, out):
    f32, f32r, bf16, i32 = mybir.dt.float32, mybir.dt.float32r, mybir.dt.bfloat16, mybir.dt.int32
    ALU, ACT, AX = mybir.AluOpType, mybir.ActivationFunctionType, mybir.AxisListType.X
    FRONT, CROSS = set(front_steps()), set(cross_steps())

    with ExitStack() as ctx:
        def sb(name, shape, dt=f32):
            return ctx.enter_context(nc.sbuf_tensor(name, shape, dt))

        scalars, used = sb("scalars", [P, 32]), iter(range(32))

        def one():
            n = next(used)
            return scalars[:, n:n + 1]

        wgu_hi, wgu_lo = (sb(n, [P, NJ, KC, 2, BW], f32r) for n in ("wgu_hi", "wgu_lo"))
        wd_hi, wd_lo = (sb(n, [P, NJ, TC, D], f32r) for n in ("wd_hi", "wd_lo"))
        gate_f = sb("gate_f", [P, KC, NE])
        gate_hi, gate_lo = (sb(n, [P, KC, NE], f32r) for n in ("gate_hi", "gate_lo"))
        con = sb("con", [P, CW])
        ident = con[:, 0:P]
        causal = con[:, P:2 * P]
        at0 = 2 * P
        cos = con[:, at0:at0 + 2 * DC]
        sin = con[:, at0 + 2 * DC:at0 + 4 * DC]
        at0 += 4 * DC
        own8 = con[:, at0:at0 + NG]
        own4 = con[:, at0 + NG:at0 + NG + HG]
        sel8 = con[:, at0 + NG + HG:at0 + 2 * NG + HG]
        ident16 = sb("ident16", [P, P], bf16)
        half, eps, zero, idle = (one() for _ in range(4))
        wc = sb("wc", [P, KC, DC])
        wback = sb("wback", [DC, D])
        wqkv_sb = sb("wqkv_sb", [DC, 5 * DC])
        gb_sb = sb("gb_sb", [DC, 2])
        bias_sb = sb("bias_sb", [P, 2, D])
        wq_sb, wo_sb = sb("wq_sb", [P, KC, D]), sb("wo_sb", [P, KC, D])
        wkv_sb = sb("wkv_sb", [P, KC, 2 * GD])
        xin, x1, x1b, xn, xnT = (sb(n, [P, D]) for n in ("xin", "x1", "x1b", "xn", "xnT"))
        x1n, x1nT = xn, xnT
        ctx_sb = sb("ctx_sb", [P, KC, P])
        mrow, mcol = sb("mrow", [P, P], i32), sb("mcol", [P, 1], i32)
        st = {n: sb("st_" + n, [P, 6]) for n in ("ln1", "lnc", "ln2", "ln3")}
        mv = {n: sb("mv_" + n, [P, 2]) for n in ("ln1", "lnc", "ln2", "ln3")}
        veps = {n: one() for n in ("ln1", "lnc", "ln2", "ln3")}
        rstd = {n: one() for n in ("ln1", "lnc", "ln2", "ln3")}
        chat, chT = sb("chat", [P, DC]), sb("chT", [DC, P])
        rope_s, qk = (sb(n, [P, 2 * DC]) for n in ("rope_s", "qk"))
        v_sb, qkT = sb("v_sb", [P, DC]), sb("qkT", [DC, 2, P])
        nmax, den, rden = (one() for _ in range(3))
        prob, probT, oT_sb = sb("prob", [P, P]), sb("probT", [P, P]), sb("oT_sb", [DC, P])
        qN = sb("qN", [P, HG, 2, GD], f32r)
        Q2 = sb("Q2", [P, HG, P], f32r)
        Q3 = sb("Q3", [96, HG, P], f32r)
        kN = sb("kN", [P, 3, GD], f32r)
        kloT = prob[0:GD, :]
        KA = sb("KA", [P, NG, P], f32r)
        KB = sb("KB", [96, NG, P], f32r)
        va = sb("va", [P, NG, HD + 1])
        padrow = sb("padrow", [P, P])
        maskn = sb("maskn", [P, P], bf16)
        padcol = one()
        negc = sb("negc", [P, P])
        PT = sb("PT", [P, NPT, HG, P])
        rdx = sb("rdx", [P, NG * HG])
        o_nat, oT2, x2, x2r = (sb(n, [P, D]) for n in ("o_nat", "oT2", "x2", "x2r"))
        x2n = o_nat
        xh, xl = sb("xh", [P, KC, P], f32r), sb("xl", [P, KC, P], f32r)
        nlmax, eall, e8 = one(), sb("eall", [P, NE]), sb("e8", [P, 8])
        tot, rtot, ksum, rk, thr = (one() for _ in range(5))
        cum = [sb(f"cum{n}", [P, 16]) for n in range(4)]
        kept, out8 = sb("kept", [P, 8]), sb("out8", [P, 8])
        ehalf, cm, ce = (sb(n, [P, NE]) for n in ("ehalf", "cm", "ce"))
        work = sb("work", [P, 4, BW])
        th, av, bv, hv = (work[:, n, :] for n in range(4))
        stage = work[:, :, :].rearrange("p (s a) n -> p s (a n)", s=2)
        hh, hl = sb("hh", [P, TC, P], f32r), sb("hl", [P, TC, P], f32r)
        y = sb("y", [P, D])
        l_tokv, l_outres = y[0:DL, :], x2r[0:DL, :]
        l_comp, l_c2l = oT2[0:DL, 0:DC], oT2[0:DL, DC:2 * DC]
        bank = [ctx.enter_context(nc.psum_tensor(f"bank{n}", [P, 512], f32)) for n in range(8)]
        G_PS, U_PS, T_PS, Y_PS, R_PS, V_PS = bank[0:6]
        RING = bank[6:8]

        PER = dict(mx=8, rmax=8, s=8, e=8, pm=8, pv=8, g=8, u=8, th=8, av=8, bv=8, h=8, T=8, hh=8, hl=8, dn=8)
        names = ("x_in ctx_in m_in w_small w_hi w_lo setup_v setup_g setup_p setup_a "
                 "st1 mv1 ve1 rs1 xb xn xnT xnT_sb c stc mvc vec rsc chat chatT chT qkv rc rsn qk v_sb qkT qkT_sb "
                 "ss smax p rden pT pT_sb oT oT_sb o1 x1 st2 mv2 ve2 rs2 x1b x1n x1nT x1nT_sb q qh ql qT Q2 Q3t "
                 "kv kh klo va kT kloT KA KB pr pr2 pc "
                 "mx rmax cT Q3c s e pm pv rdx on oT2 oT2_sb wo x2 st3 mv3 ve3 rs3 x2n "
                 "x2r xT xh xl lg nlmax eall eh e8 tot rtot cu0 cu1 cu2 cu3 ksum out8a out8b thr rk cm ce "
                 "g u th av bv h T hh hl dn y out").split()
        S = {n: ctx.enter_context(nc.semaphore("s_" + n)) for n in names}
        S["w_in"] = [ctx.enter_context(nc.semaphore(f"s_w_in{n}")) for n in range(2)]

        def nth(name, b, k=1):
            return b * PER.get(name, 1) + k

        block = ctx.enter_context(nc.Block())

        def piece_of(gu, dn, j, n):
            return gu[:, j, n, :, :].rearrange("p g n -> p (g n)") if n < KC else dn[:, j, :, :].rearrange("p t n -> p (t n)")

        def is_first(b):
            return isinstance(b, int) and b == 0

        def schedule(eng, steps):
            def iteration(i, front, cross):
                for s in ORDER:
                    if s in FRONT:
                        if front and s in steps:
                            steps[s](i + 2)
                    elif s in CROSS:
                        if cross and s in steps:
                            steps[s](i + 1)
                    elif s in steps:
                        steps[s](i)

            cs = cross_steps()
            for n, s in enumerate(front_steps()):
                if s in steps:
                    steps[s](0)
                if n % 3 == 2 and "split" in steps and n // 3 < 3:
                    steps["split"](n // 3)
            for n in range(19):
                s = front_steps()[n]
                for c in cs[n * len(cs) // 16:(n + 1) * len(cs) // 16] if n < 16 else []:
                    if c in steps:
                        steps[c](0)
                if s in steps:
                    steps[s](1)
                if n % 3 == 2 and "split" in steps and 3 + n // 3 < NJ:
                    steps["split"](3 + n // 3)
            iteration(0, True, True)
            with eng.Fori(1, NB - 2) as i:
                iteration(i, True, True)
            iteration(NB - 2, False, True)
            iteration(NB - 1, False, False)

        def row(t, b):
            if isinstance(b, int):
                return t[b]
            return t[bass.ds(b, 1)].squeeze(0)

        @block.sync
        def _(sp):
            for dst, src in ((con[:, :], consts), (l_tokv, wtokv), (l_outres, woutresT), (l_comp, wcompT),
                             (l_c2l, wc2l), (wqkv_sb[:, :], wqkv), (gb_sb[:, :], gb), (bias_sb[:, :, :], bias2),
                             (wq_sb[:, :, :], wq), (wkv_sb[:, :, :], wkv), (wo_sb[:, :, :], wo), (gate_f[:, :, :], gateT)):
                sp.dma_start(dst, src).then_inc(S["w_small"], 16)

            def load_batch(b):
                if not is_first(b):
                    sp.wait_ge(S["x1"], nth("x1", b - 1))
                sp.dma_start(xin[:, :], row(x, b)).then_inc(S["x_in"], 16)
                if not is_first(b):
                    sp.wait_ge(S["kv"], nth("kv", b - 1))
                    sp.wait_ge(S["pr"], nth("pr", b - 1))
                    sp.wait_ge(S["pc"], nth("pc", b - 1))
                sp.dma_start(ctx_sb[:, :, :], row(ctxT, b)).then_inc(S["ctx_in"], 16)
                sp.dma_start(mrow[:, :], row(mask, b).partition_broadcast(P)).then_inc(S["m_in"], 16)
                sp.dma_start(mcol[:, :], row(mask, b).rearrange("(p o) -> p o", o=1)).then_inc(S["m_in"], 16)

            def load_split(j):
                for n in range(3):
                    piece = 3 * j + n
                    if piece >= 2:
                        sp.wait_ge(S["w_lo"], piece - 1)
                    src = wgu[:, j, n * PW:(n + 1) * PW] if n < KC else wd[:, j, :]
                    sp.dma_start(stage[:, piece % 2, :], src).then_inc(S["w_in"][piece % 2], 16)

            def store(b):
                sp.wait_ge(S["y"], nth("y", b))
                sp.dma_start(row(out, b), y[:, :]).then_inc(S["out"], 16)

            def r1(b):
                if isinstance(b, int) and b < 2:
                    load_batch(b)

            def xT(i):
                if not isinstance(i, int) or i + 2 < NB:
                    load_batch(i + 2)

            schedule(sp, {"r1": r1, "xT": xT, "split": load_split, "y": store})
            sp.wait_ge(S["out"], 16 * NB)

        @block.gpsimd
        def _(pool):
            gp = nc.gpsimd

            def landed():
                gp.tensor_tensor(idle[:, :], zero[:, :], zero[:, :], ALU.add)
            gp.memset(half[:, :], -0.5).then_inc(S["setup_g"], 1)
            gp.memset(eps[:, :], EPS).then_inc(S["setup_g"], 1)
            gp.memset(zero[:, :], 0.0).then_inc(S["setup_g"], 1)
            gp.memset(negc[:, :], 0.0).then_inc(S["setup_g"], 1)
            gp.memset(va[:, :, HD:HD + 1], 1.0).then_inc(S["setup_g"], 1)
            for c in cum:
                gp.memset(c[:, 0:8], 0.0).then_inc(S["setup_g"], 1)
            pool.wait_ge(S["w_small"], 12 * 16)
            gp.tensor_copy(ident16[:, :], ident).then_inc(S["setup_g"], 1)
            pool.wait_ge(S["setup_g"], 3)

            def inv_std(ln, sm, sv, sr, b):
                pool.wait_ge(S[sm], nth(sm, b))
                gp.tensor_tensor(veps[ln][:, :], mv[ln][:, 1:2], eps[:, :], ALU.add).then_inc(S[sv], 1)
                pool.wait_ge(S[sv], nth(sv, b))
                gp.tensor_tensor(rstd[ln][:, :], veps[ln][:, :], half[:, :], ALU.pow).then_inc(S[sr], 1)

            def r1(b):
                inv_std("ln1", "mv1", "ve1", "rs1", b)

            def r2(b):
                pool.wait_ge(S["xn"], nth("xn", b))
                gp.tensor_tensor(xin[:, :], xin[:, :], bias_sb[:, 0, :], ALU.add).then_inc(S["xb"], 1)

            def r4(b):
                inv_std("lnc", "mvc", "vec", "rsc", b)

            def r13(b):
                inv_std("ln2", "mv2", "ve2", "rs2", b)

            def r17(b):
                pool.wait_ge(S["x1"], nth("x1", b))
                if not is_first(b):
                    pool.wait_ge(S["x2"], nth("x2", b - 1))
                gp.tensor_tensor(x1b[:, :], x1[:, :], bias_sb[:, 1, :], ALU.add).then_inc(S["x1b"], 1)
                pool.wait_ge(S["Q2"], nth("Q2", b))
                gp.tensor_tensor(Q3[0:GD, :, :], Q2[0:GD, :, :].bitcast(f32), zero[0:GD, :].unsqueeze(2).to_broadcast([GD, HG, P]),
                                 ALU.add).then_inc(S["Q3t"], 1)

            def r18(b):
                if not is_first(b):
                    pool.wait_ge(S["mx"], nth("mx", b - 1, 8))
                pool.wait_ge(S["pr"], nth("pr", b))
                gp.tensor_tensor(maskn[:, :], padrow[:, :], causal, ALU.add).then_inc(S["pr2"], 1)

            def r19(b):
                pool.wait_ge(S["kloT"], nth("kloT", b))
                if not is_first(b):
                    pool.wait_ge(S["s"], nth("s", b - 1, 8))
                gp.tensor_tensor(KB[0:GD, :, :], kloT.unsqueeze(1).to_broadcast([GD, NG, P]),
                                 own8[0:GD, :].unsqueeze(2).to_broadcast([GD, NG, P]), ALU.mult).then_inc(S["KB"], 1)

            def s_(g):
                def f(b):
                    if g > 0:
                        pool.wait_ge(S["pm"], nth("pm", b, g))
                    elif not is_first(b):
                        pool.wait_ge(S["pm"], nth("pm", b - 1, NG))
                    pool.wait_ge(S["e"], nth("e", b, g + 1))
                    landed()
                    gp.affine_select(out=PT[:, g % NPT, :, :], in_=PT[:, g % NPT, :, :], compare_op=ALU.is_ge, fill=0.0, base=0,
                                     pattern=[[0, HG], [1, P]], channel_multiplier=-1).then_inc(S["pm"], 1)
                return f

            def wo_(b):
                inv_std("ln3", "mv3", "ve3", "rs3", b)

            def xT(b):
                pool.wait_ge(S["x2"], nth("x2", b))
                if not is_first(b):
                    pool.wait_ge(S["y"], nth("y", b - 1))
                gp.tensor_tensor(x2r[:, :], x2[:, :], zero[:, :].to_broadcast([P, D]), ALU.add).then_inc(S["x2r"], 1)

            def ab(j):
                def f(b):
                    pool.wait_ge(S["bv"], nth("bv", b, j + 1))
                    pool.wait_ge(S["ce"], nth("ce", b))
                    if j > 0:
                        pool.wait_ge(S["T"], nth("T", b, j))
                    elif not is_first(b):
                        pool.wait_ge(S["T"], nth("T", b - 1, NJ))
                    gp.tensor_tensor(hv.rearrange("p (e i) -> p e i", e=EJ), bv.rearrange("p (e i) -> p e i", e=EJ),
                                     ce[:, EJ * j:EJ * j + EJ].unsqueeze(2).to_broadcast([P, EJ, NI]), ALU.mult).then_inc(S["h"], 1)
                return f

            schedule(pool, {"r1": r1, "r2": r2, "r4": r4, "r13": r13, "r17": r17, "r18": r18, "r19": r19, "wo": wo_, "xT": xT,
                            **{f"s{g}": s_(g) for g in range(NG)}, **{f"ab{j}": ab(j) for j in range(NJ)}})

        @block.scalar
        def _(act):
            ac = nc.scalar

            def copy(o, i):
                return ac.activation(o, i, ACT.Copy)

            act.wait_ge(S["setup_p"], 2)
            copy(wc[:, :, :], R_PS[:, 0:KC * DC].rearrange("p (k c) -> p k c", k=KC)).then_inc(S["setup_a"], 1)
            copy(wback[:, :], R_PS[0:DC, 128:128 + D]).then_inc(S["setup_a"], 1)
            copy(gate_hi[:, :, :], gate_f[:, :, :]).then_inc(S["setup_a"], 1)
            copy(KB[GD:96, :, :], sel8[GD:96, :].unsqueeze(2).to_broadcast([32, NG, P])).then_inc(S["setup_a"], 1)

            def split(j):
                for n in range(3):
                    piece = 3 * j + n
                    act.wait_ge(S["w_in"][piece % 2], 16 * (piece // 2 + 1))
                    copy(piece_of(wgu_hi, wd_hi, j, n), stage[:, piece % 2, :]).then_inc(S["w_hi"], 1)

            def r3(b):
                act.wait_ge(S["xnT"], nth("xnT", b))
                copy(xnT[:, :], R_PS[:, 0:D]).then_inc(S["xnT_sb"], 1)

            def r8(b):
                act.wait_ge(S["qkT"], nth("qkT", b))
                copy(qkT[:, :, :], R_PS[0:DC, 0:2 * P].rearrange("p (a n) -> p a n", a=2)).then_inc(S["qkT_sb"], 1)

            def r10(b):
                act.wait_ge(S["smax"], nth("smax", b))
                ac.activation(prob[:, :], R_PS[:, 0:P], ACT.Exp, bias=nmax[:, :], accum_out=den[:, :]).then_inc(S["p"], 1)

            def r11(b):
                act.wait_ge(S["pT"], nth("pT", b))
                copy(probT[:, :], R_PS[:, 0:P]).then_inc(S["pT_sb"], 1)

            def r12(b):
                act.wait_ge(S["oT"], nth("oT", b))
                copy(oT_sb[:, :], R_PS[0:DC, 0:P]).then_inc(S["oT_sb"], 1)

            def r15(b):
                act.wait_ge(S["x1nT"], nth("x1nT", b))
                copy(x1nT[:, :], R_PS[:, 0:D]).then_inc(S["x1nT_sb"], 1)

            def r16(b):
                act.wait_ge(S["q"], nth("q", b))
                copy(qN[:, :, 0, :], R_PS[:, 0:D].rearrange("p (h c) -> p h c", h=HG)).then_inc(S["qh"], 1)

            def r17(b):
                act.wait_ge(S["qT"], nth("qT", b))
                if not is_first(b):
                    act.wait_ge(S["s"], nth("s", b - 1, 8))
                copy(Q2[:, :, :], R_PS[:, :].rearrange("p (h n) -> p h n", h=HG)).then_inc(S["Q2"], 1)

            def r18(b):
                act.wait_ge(S["kv"], nth("kv", b))
                copy(kN[:, 0:2, :], R_PS[:, 0:GD].unsqueeze(1).to_broadcast([P, 2, GD])).then_inc(S["kh"], 1)
                if is_first(b):
                    act.wait_ge(S["setup_g"], 5)
                else:
                    act.wait_ge(S["pv"], nth("pv", b - 1, 8))
                copy(va[:, :, 0:HD], R_PS[:, GD:2 * GD].rearrange("p (g d) -> p g d", g=NG)).then_inc(S["va"], 1)

            def r19(b):
                act.wait_ge(S["kT"], nth("kT", b))
                if not is_first(b):
                    act.wait_ge(S["KB"], nth("KB", b - 1))
                copy(kloT, R_PS[0:GD, P:2 * P]).then_inc(S["kloT"], 1)

            def s_(g):
                def f(b):
                    act.wait_ge(S["s"], nth("s", b, g + 1))
                    if g == 0:
                        act.wait_ge(S["pc"], nth("pc", b))
                    ac.activation(PT[:, g % NPT, :, :].rearrange("p h n -> p (h n)"), RING[(9 + g) % 2][:, :], ACT.Exp,
                                  bias=padcol[:, :], scale=float(HD) ** -0.5).then_inc(S["e"], 1)
                return f

            def oT_(b):
                act.wait_ge(S["oT2"], nth("oT2", b))
                copy(oT2[:, :], RING[17 % 2][:, 0:D]).then_inc(S["oT2_sb"], 1)

            def xT(b):
                act.wait_ge(S["xT"], nth("xT", b))
                copy(xh[:, :, :], T_PS[:, 0:D].rearrange("p (k n) -> p k n", k=KC)).then_inc(S["xh"], 1)

            def gate1(b):
                act.wait_ge(S["nlmax"], nth("nlmax", b))
                ac.activation(eall[:, :], Y_PS[:, 0:NE], ACT.Exp, bias=nlmax[:, :]).then_inc(S["eall"], 1)

            def gu(j):
                def f(b):
                    act.wait_ge(S["g"], nth("g", b, j + 1))
                    ac.activation(th, G_PS[:, 0:BW], ACT.Tanh, scale=0.5).then_inc(S["th"], 1)
                return f

            def T_(j):
                def f(b):
                    act.wait_ge(S["T"], nth("T", b, j + 1))
                    copy(hh[:, :, :], T_PS[:, 0:BW].rearrange("p (t n) -> p t n", t=TC)).then_inc(S["hh"], 1)
                return f

            schedule(act, {"split": split, "r3": r3, "r8": r8, "r10": r10, "r11": r11, "r12": r12, "r15": r15,
                           "r16": r16, "r17": r17, "r18": r18, "r19": r19, "oT": oT_, "xT": xT, "gate1": gate1,
                           **{f"s{g}": s_(g) for g in range(NG)},
                           **{f"gu{j}": gu(j) for j in range(NJ)}, **{f"T{j}": T_(j) for j in range(NJ)}})

        @block.vector
        def _(dve):
            v = nc.vector
            dve.wait_ge(S["w_small"], 12 * 16)
            v.tensor_tensor(l_outres, l_outres, l_tokv, ALU.add).then_inc(S["setup_v"], 1)
            dve.wait_ge(S["setup_a"], 3)
            v.tensor_tensor(gate_lo[:, :, :], gate_f[:, :, :], gate_hi[:, :, :].bitcast(f32), ALU.subtract).then_inc(S["setup_v"], 1)

            def stats(ln, src, ss, sm, b):
                v.bn_stats(st[ln][:, :], src).then_inc(S[ss], 1)
                dve.drain()
                v.bn_aggr(mv[ln][:, :], st[ln][:, :]).then_inc(S[sm], 1)

            def normal(ln, o, src):
                return v.tensor_scalar(o, src, mv[ln][:, 0:1], rstd[ln][:, :], ALU.subtract, ALU.mult)

            def split(j):
                for n in range(3):
                    piece = 3 * j + n
                    dve.wait_ge(S["w_hi"], piece + 1)
                    v.tensor_tensor(piece_of(wgu_lo, wd_lo, j, n), stage[:, piece % 2, :],
                                    piece_of(wgu_hi, wd_hi, j, n).bitcast(f32), ALU.subtract).then_inc(S["w_lo"], 1)

            def r1(b):
                dve.wait_ge(S["x_in"], 16 * b + 16)
                stats("ln1", xin[:, :], "st1", "mv1", b)

            def r2(b):
                dve.wait_ge(S["rs1"], nth("rs1", b))
                normal("ln1", xn[:, :], xin[:, :]).then_inc(S["xn"], 1)

            def r4(b):
                dve.wait_ge(S["c"], nth("c", b))
                stats("lnc", R_PS[:, 0:DC], "stc", "mvc", b)

            def r5(b):
                dve.wait_ge(S["rsc"], nth("rsc", b))
                normal("lnc", chat[:, :], R_PS[:, 0:DC]).then_inc(S["chat"], 1)

            def r6(b):
                dve.wait_ge(S["chatT"], nth("chatT", b))
                v.tensor_scalar(chT[:, :], R_PS[0:DC, 0:P], gb_sb[:, 0:1], gb_sb[:, 1:2], ALU.mult, ALU.add).then_inc(S["chT"], 1)

            def r7(b):
                dve.wait_ge(S["qkv"], nth("qkv", b))
                v.tensor_tensor(qk[:, :], R_PS[:, 0:2 * DC], cos, ALU.mult).then_inc(S["rc"], 1)
                v.tensor_tensor(rope_s[:, :], R_PS[:, 2 * DC:4 * DC], sin, ALU.mult).then_inc(S["rsn"], 1)
                v.tensor_copy(v_sb[:, :], R_PS[:, 4 * DC:5 * DC]).then_inc(S["v_sb"], 1)
                dve.wait_ge(S["rc"], nth("rc", b))
                dve.wait_ge(S["rsn"], nth("rsn", b))
                v.tensor_tensor(qk[:, :], qk[:, :], rope_s[:, :], ALU.add).then_inc(S["qk"], 1)

            def r9(b):
                dve.wait_ge(S["ss"], nth("ss", b))
                v.tensor_reduce(nmax[:, :], R_PS[:, 0:P], AX, ALU.max, negate=True).then_inc(S["smax"], 1)

            def r10(b):
                dve.wait_ge(S["p"], nth("p", b))
                v.reciprocal(rden[:, :], den[:, :]).then_inc(S["rden"], 1)

            def r13(b):
                dve.wait_ge(S["o1"], nth("o1", b))
                dve.wait_ge(S["rden"], nth("rden", b))
                dve.wait_ge(S["xb"], nth("xb", b))
                if not is_first(b):
                    dve.wait_ge(S["x1b"], nth("x1b", b - 1))
                v.scalar_tensor_tensor(x1[:, :], R_PS[:, 0:D], rden[:, :], xin[:, :], ALU.mult, ALU.add).then_inc(S["x1"], 1)
                dve.wait_ge(S["x1"], nth("x1", b))
                stats("ln2", x1[:, :], "st2", "mv2", b)

            def r14(b):
                dve.wait_ge(S["rs2"], nth("rs2", b))
                normal("ln2", x1n[:, :], x1[:, :]).then_inc(S["x1n"], 1)

            def r16(b):
                dve.wait_ge(S["qh"], nth("qh", b))
                v.tensor_tensor(qN[:, :, 1, :], R_PS[:, 0:D].rearrange("p (h c) -> p h c", h=HG),
                                qN[:, :, 0, :].bitcast(f32), ALU.subtract).then_inc(S["ql"], 1)

            def r18(b):
                dve.wait_ge(S["m_in"], 32 * b + 32)
                if not is_first(b):
                    dve.wait_ge(S["pr2"], nth("pr2", b - 1))
                v.tensor_scalar(padrow[:, :], mrow[:, :], 0.0, -BIG, ALU.is_equal, ALU.mult).then_inc(S["pr"], 1)
                if not is_first(b):
                    dve.wait_ge(S["e"], nth("e", b - 1, 8))
                v.tensor_scalar(padcol[:, :], mcol[:, :], 0.0, -BIG, ALU.is_equal, ALU.mult).then_inc(S["pc"], 1)
                dve.wait_ge(S["va"], nth("va", b))
                v.tensor_tensor(kN[:, 2, :], R_PS[:, 0:GD], kN[:, 0, :].bitcast(f32), ALU.subtract).then_inc(S["klo"], 1)

            def r19(b):
                dve.wait_ge(S["kloT"], nth("kloT", b))
                if not is_first(b):
                    dve.wait_ge(S["s"], nth("s", b - 1, 8))
                v.tensor_tensor(KA[:, :, :], R_PS[:, 0:P].unsqueeze(1).to_broadcast([P, NG, P]),
                                own8.unsqueeze(2).to_broadcast([P, NG, P]), ALU.mult).then_inc(S["KA"], 1)

            def mx(u):
                hg, hf = u % HG, u // HG
                def f(b):
                    if u == 0 and is_first(b):
                        dve.wait_ge(S["setup_g"], 4)
                    dve.wait_ge(S["mx"], nth("mx", b, u + 1))
                    at = GD + 16 * hf + hg
                    v.tensor_reduce(negc[:, at:at + 13:HG], RING[u % 2][:, :].rearrange("p (g m) -> p g m", g=HG), AX, ALU.max,
                                    negate=True).then_inc(S["rmax"], 1)
                return f

            def c(b):
                dve.wait_ge(S["cT"], nth("cT", b))
                v.tensor_tensor(Q3[GD:96, :, :], RING[8 % 2][GD:96, 0:P].unsqueeze(1).to_broadcast([32, HG, P]),
                                own4[GD:96, :].unsqueeze(2).to_broadcast([32, HG, P]), ALU.mult).then_inc(S["Q3c"], 1)

            def on(b):
                heads = V_PS[:, 0:NG * HG * (HD + 1)].rearrange("p (h d) -> p h d", d=HD + 1)
                dve.wait_ge(S["pv"], nth("pv", b, 8))
                v.reciprocal(rdx[:, :].unsqueeze(2), heads[:, :, HD:HD + 1]).then_inc(S["rdx"], 1)
                dve.wait_ge(S["rdx"], nth("rdx", b))
                v.tensor_tensor(o_nat[:, :].rearrange("p (h d) -> p h d", d=HD), heads[:, :, 0:HD],
                                rdx[:, :].unsqueeze(2).to_broadcast([P, NG * HG, HD]), ALU.mult).then_inc(S["on"], 1)

            def wo_(b):
                dve.wait_ge(S["wo"], nth("wo", b))
                dve.wait_ge(S["x1b"], nth("x1b", b))
                if not is_first(b):
                    dve.wait_ge(S["x2r"], nth("x2r", b - 1))
                v.tensor_tensor(x2[:, :], RING[18 % 2][:, 0:D], x1b[:, :], ALU.add).then_inc(S["x2"], 1)
                dve.wait_ge(S["x2"], nth("x2", b))
                stats("ln3", x2[:, :], "st3", "mv3", b)

            def n3(b):
                dve.wait_ge(S["rs3"], nth("rs3", b))
                normal("ln3", x2n[:, :], x2[:, :]).then_inc(S["x2n"], 1)

            def xT(b):
                dve.wait_ge(S["xh"], nth("xh", b))
                v.tensor_tensor(xl[:, :, :], T_PS[:, 0:D].rearrange("p (k n) -> p k n", k=KC), xh[:, :, :].bitcast(f32),
                                ALU.subtract).then_inc(S["xl"], 1)

            def gate1(b):
                dve.wait_ge(S["lg"], nth("lg", b))
                v.tensor_reduce(nlmax[:, :], Y_PS[:, 0:NE], AX, ALU.max, negate=True).then_inc(S["nlmax"], 1)

            def gate2(b):
                if is_first(b):
                    dve.wait_ge(S["setup_g"], 9)
                dve.wait_ge(S["eall"], nth("eall", b))
                v.tensor_scalar(ehalf[:, :], eall[:, :], 0.5, None, ALU.mult).then_inc(S["eh"], 1)
                v.max(e8[:, :], eall[:, :]).then_inc(S["e8"], 1)
                dve.wait_ge(S["e8"], nth("e8", b))
                v.reduce_sum(tot[:, :], e8[:, :], AX).then_inc(S["tot"], 1)
                dve.wait_ge(S["tot"], nth("tot", b))
                v.reciprocal(rtot[:, :], tot[:, :]).then_inc(S["rtot"], 1)
                dve.wait_ge(S["rtot"], nth("rtot", b))
                v.tensor_scalar(cum[0][:, 8:16], e8[:, :], rtot[:, :], None, ALU.mult).then_inc(S["cu0"], 1)
                for n, by in enumerate((1, 2, 4)):
                    dve.wait_ge(S[f"cu{n}"], nth(f"cu{n}", b))
                    v.tensor_tensor(cum[n + 1][:, 8:16], cum[n][:, 8:16], cum[n][:, 8 - by:16 - by], ALU.add).then_inc(S[f"cu{n + 1}"], 1)
                dve.wait_ge(S["cu3"], nth("cu3", b))
                v.scalar_tensor_tensor(kept[:, :], cum[3][:, 7:15], KEEP, e8[:, :], ALU.is_lt, ALU.mult,
                                       accum_out=ksum[:, :]).then_inc(S["ksum"], 1)
                v.tensor_scalar(out8[:, :], cum[3][:, 7:15], KEEP, 4.0, ALU.is_ge, ALU.mult).then_inc(S["out8a"], 1)
                dve.wait_ge(S["out8a"], nth("out8a", b))
                v.tensor_tensor(out8[:, :], out8[:, :], e8[:, :], ALU.add).then_inc(S["out8b"], 1)
                dve.wait_ge(S["out8b"], nth("out8b", b))
                v.tensor_reduce(thr[:, :], out8[:, :], AX, ALU.min).then_inc(S["thr"], 1)
                dve.wait_ge(S["ksum"], nth("ksum", b))
                v.reciprocal(rk[:, :], ksum[:, :]).then_inc(S["rk"], 1)
                dve.wait_ge(S["thr"], nth("thr", b))
                dve.wait_ge(S["eh"], nth("eh", b))
                v.scalar_tensor_tensor(cm[:, :], eall[:, :], thr[:, :], ehalf[:, :], ALU.is_ge, ALU.mult).then_inc(S["cm"], 1)
                dve.wait_ge(S["cm"], nth("cm", b))
                dve.wait_ge(S["rk"], nth("rk", b))
                v.tensor_scalar(ce[:, :], cm[:, :], rk[:, :], None, ALU.mult).then_inc(S["ce"], 1)

            def ab(j):
                def f(b):
                    dve.wait_ge(S["th"], nth("th", b, j + 1))
                    v.scalar_tensor_tensor(av, th, 1.0, G_PS[:, 0:BW], ALU.add, ALU.mult).then_inc(S["av"], 1)
                    dve.wait_ge(S["av"], nth("av", b, j + 1))
                    dve.wait_ge(S["u"], nth("u", b, j + 1))
                    if j > 0:
                        dve.wait_ge(S["h"], nth("h", b, j))
                    elif not is_first(b):
                        dve.wait_ge(S["h"], nth("h", b - 1, NJ))
                    v.tensor_tensor(bv, av, U_PS[:, 0:BW], ALU.mult).then_inc(S["bv"], 1)
                return f

            def T_(j):
                def f(b):
                    dve.wait_ge(S["hh"], nth("hh", b, j + 1))
                    v.tensor_tensor(hl[:, :, :], T_PS[:, 0:BW].rearrange("p (t n) -> p t n", t=TC), hh[:, :, :].bitcast(f32),
                                    ALU.subtract).then_inc(S["hl"], 1)
                return f

            def y_(b):
                dve.wait_ge(S["dn"], nth("dn", b, NJ))
                dve.wait_ge(S["x2r"], nth("x2r", b))
                if not is_first(b):
                    dve.wait_ge(S["out"], 16 * b)
                v.tensor_tensor(y[:, :], Y_PS[:, 0:D], x2r[:, :], ALU.add).then_inc(S["y"], 1)

            schedule(dve, {"split": split, "r1": r1, "r2": r2, "r4": r4, "r5": r5, "r6": r6, "r7": r7, "r9": r9, "r10": r10,
                           "r13": r13, "r14": r14, "r16": r16, "r18": r18, "r19": r19,
                           **{f"mx{u}": mx(u) for u in range(8)}, "c": c, "on": on, "wo": wo_, "n3": n3, "xT": xT,
                           "gate1": gate1, "gate2": gate2, "y": y_,
                           **{f"ab{j}": ab(j) for j in range(NJ)}, **{f"T{j}": T_(j) for j in range(NJ)}})

        @block.tensor
        def _(pe):
            t = nc.tensor
            pe.wait_ge(S["w_small"], 12 * 16)
            for k in range(KC):
                last = t.matmul(R_PS[:, k * DC:(k + 1) * DC], l_tokv[:, k * P:(k + 1) * P], l_comp, start=True, stop=True)
            last.then_inc(S["setup_p"], 1)
            pe.wait_ge(S["setup_v"], 1)
            t.matmul(R_PS[0:DC, 128:128 + D], l_c2l, l_outres, start=True, stop=True).then_inc(S["setup_p"], 1)

            def halves(o, src):
                for k in range(KC):
                    last = t.transpose(o[:, k * P:(k + 1) * P], src[:, k * P:(k + 1) * P], ident)
                return last

            def product(o, xT, w):
                for k in range(KC):
                    last = t.matmul(o, xT[:, k * P:(k + 1) * P], w[:, k, :], start=k == 0, stop=k == KC - 1)
                return last

            def r3(b):
                if is_first(b):
                    pe.wait_ge(S["setup_a"], 2)
                else:
                    pe.wait_ge(S["KA"], nth("KA", b - 1))
                    pe.wait_ge(S["kloT"], nth("kloT", b - 1))
                pe.wait_ge(S["xn"], nth("xn", b))
                halves(R_PS, xn).then_inc(S["xnT"], 1)

            def r4(b):
                pe.wait_ge(S["xnT_sb"], nth("xnT_sb", b))
                product(R_PS[:, 0:DC], xnT, wc).then_inc(S["c"], 1)

            def r6(b):
                pe.wait_ge(S["chat"], nth("chat", b))
                t.transpose(R_PS[0:DC, 0:P], chat[:, :], ident).then_inc(S["chatT"], 1)

            def r7(b):
                pe.wait_ge(S["chT"], nth("chT", b))
                t.matmul(R_PS[:, 0:5 * DC], chT[:, :], wqkv_sb[:, :], start=True, stop=True).then_inc(S["qkv"], 1)

            def r8(b):
                pe.wait_ge(S["qk"], nth("qk", b))
                pe.wait_ge(S["v_sb"], nth("v_sb", b))
                for a in range(2):
                    last = t.transpose(R_PS[0:DC, a * P:(a + 1) * P], qk[:, a * DC:(a + 1) * DC], ident)
                last.then_inc(S["qkT"], 1)

            def r9(b):
                pe.wait_ge(S["qkT_sb"], nth("qkT_sb", b))
                t.matmul(R_PS[:, 0:P], qkT[:, 0, :], qkT[:, 1, :], start=True, stop=False)
                t.matmul(R_PS[:, 0:P], ident, causal, start=False, stop=True).then_inc(S["ss"], 1)

            def r11(b):
                pe.wait_ge(S["p"], nth("p", b))
                t.transpose(R_PS[:, 0:P], prob[:, :], ident).then_inc(S["pT"], 1)

            def r12(b):
                pe.wait_ge(S["pT_sb"], nth("pT_sb", b))
                t.matmul(R_PS[0:DC, 0:P], v_sb[:, :], probT[:, :], start=True, stop=True).then_inc(S["oT"], 1)

            def r13(b):
                pe.wait_ge(S["oT_sb"], nth("oT_sb", b))
                t.matmul(R_PS[:, 0:D], oT_sb[:, :], wback[:, :], start=True, stop=True).then_inc(S["o1"], 1)

            def r15(b):
                pe.wait_ge(S["x1n"], nth("x1n", b))
                halves(R_PS, x1n).then_inc(S["x1nT"], 1)

            def r16(b):
                pe.wait_ge(S["x1nT_sb"], nth("x1nT_sb", b))
                product(R_PS[:, 0:D], x1nT, wq_sb).then_inc(S["q"], 1)

            def r17(b):
                pe.wait_ge(S["qh"], nth("qh", b))
                pe.wait_ge(S["ql"], nth("ql", b))
                for h in range(HG):
                    last = t.transpose(R_PS[:, h * P:(h + 1) * P], qN[:, h, :, :].rearrange("p a c -> p (a c)").bitcast(f32), ident)
                last.then_inc(S["qT"], 1)

            def r18(b):
                pe.wait_ge(S["Q2"], nth("Q2", b))
                pe.wait_ge(S["ctx_in"], 16 * b + 16)
                for k in range(KC):
                    last = t.matmul(R_PS[:, 0:2 * GD], ctx_sb[:, k, :], wkv_sb[:, k, :], start=k == 0, stop=k == KC - 1)
                last.then_inc(S["kv"], 1)

            def r19(b):
                pe.wait_ge(S["kh"], nth("kh", b))
                pe.wait_ge(S["klo"], nth("klo", b))
                pe.wait_ge(S["va"], nth("va", b))
                t.transpose(R_PS[:, 0:P], kN[:, 0:2, :].rearrange("p a c -> p (a c)").bitcast(f32), ident)
                t.transpose(R_PS[0:GD, P:2 * P], kN[:, 2, :].bitcast(f32), ident).then_inc(S["kT"], 1)

            READ = ([("rmax", u + 1) for u in range(8)] + [("Q3c", 1)] + [("e", g + 1) for g in range(NG)]
                    + [("oT2_sb", 1), ("x2", 1)])

            def ring_free(use, b):
                if use >= 2:
                    n, k = READ[use - 2]
                    pe.wait_ge(S[n], nth(n, b, k))
                elif not is_first(b):
                    n, k = READ[max(u for u in range(len(READ)) if u % 2 == use)]
                    pe.wait_ge(S[n], nth(n, b - 1, k))

            def mx(u):
                hg, hf = u % HG, u // HG
                def f(b):
                    ring_free(u, b)
                    if u == 0:
                        if is_first(b):
                            pe.wait_ge(S["setup_g"], 10)
                        pe.wait_ge(S["KA"], nth("KA", b))
                        pe.wait_ge(S["Q2"], nth("Q2", b))
                        pe.wait_ge(S["pr2"], nth("pr2", b))
                    o = RING[u % 2]
                    t.matmul(o[:, :], Q2[:, hg, :], KA[:, HG * hf:HG * hf + HG, :].rearrange("p g m -> p (g m)"), start=True, stop=False)
                    t.matmul(o[:, :], ident16[:, :], maskn[:, :].unsqueeze(1).to_broadcast([P, HG, P]), start=False, stop=True).then_inc(S["mx"], 1)
                return f

            def c(b):
                ring_free(8, b)
                pe.wait_ge(S["rmax"], nth("rmax", b, 8))
                t.transpose(RING[8 % 2][:, 0:P], negc[:, :], ident).then_inc(S["cT"], 1)

            def s_(g):
                def f(b):
                    ring_free(9 + g, b)
                    if g == 0:
                        pe.wait_ge(S["Q3c"], nth("Q3c", b))
                        pe.wait_ge(S["Q3t"], nth("Q3t", b))
                        pe.wait_ge(S["KB"], nth("KB", b))
                        if is_first(b):
                            pe.wait_ge(S["setup_a"], 4)
                    o = RING[(9 + g) % 2]
                    t.matmul(o[:, :], KA[:, g, :], Q2[:, :, :].rearrange("p h n -> p (h n)"), start=True, stop=False)
                    t.matmul(o[:, :], KB[:, g, :], Q3[:, :, :].rearrange("p h n -> p (h n)"), start=False, stop=True).then_inc(S["s"], 1)
                return f

            def pv(g):
                def f(b):
                    if g == 0 and not is_first(b):
                        pe.wait_ge(S["on"], nth("on", b - 1))
                    pe.wait_ge(S["pm"], nth("pm", b, g + 1))
                    for h in range(HG):
                        at = (g * HG + h) * (HD + 1)
                        last = t.matmul(V_PS[:, at:at + HD + 1], PT[:, g % NPT, h, :], va[:, g, :], start=True, stop=True)
                    last.then_inc(S["pv"], 1)
                return f

            def oT_(b):
                ring_free(17, b)
                pe.wait_ge(S["on"], nth("on", b))
                halves(RING[17 % 2], o_nat).then_inc(S["oT2"], 1)

            def wo_(b):
                ring_free(18, b)
                pe.wait_ge(S["oT2_sb"], nth("oT2_sb", b))
                product(RING[18 % 2][:, 0:D], oT2, wo_sb).then_inc(S["wo"], 1)

            def xT(b):
                if not is_first(b):
                    pe.wait_ge(S["hl"], nth("hl", b - 1, NJ))
                pe.wait_ge(S["x2n"], nth("x2n", b))
                halves(T_PS, x2n).then_inc(S["xT"], 1)

            def three(o, hi, lo, whi, wlo, first, last_):
                t.matmul(o, hi, whi, start=first, stop=False)
                t.matmul(o, hi, wlo, start=False, stop=False)
                return t.matmul(o, lo, whi, start=False, stop=last_)

            def lg(b):
                if is_first(b):
                    pe.wait_ge(S["setup_v"], 2)
                else:
                    pe.wait_ge(S["y"], nth("y", b - 1))
                pe.wait_ge(S["xl"], nth("xl", b))
                for k in range(KC):
                    last = three(Y_PS[:, 0:NE], xh[:, k, :], xl[:, k, :], gate_hi[:, k, :], gate_lo[:, k, :], k == 0, k == KC - 1)
                last.then_inc(S["lg"], 1)

            def gu(j):
                def f(b):
                    if is_first(b):
                        pe.wait_ge(S["w_lo"], 3 * j + 3)
                    if j > 0:
                        pe.wait_ge(S["av"], nth("av", b, j))
                    elif not is_first(b):
                        pe.wait_ge(S["av"], nth("av", b - 1, NJ))
                    for k in range(KC):
                        last = three(G_PS[:, 0:BW], xh[:, k, :], xl[:, k, :], wgu_hi[:, j, k, 0, :], wgu_lo[:, j, k, 0, :],
                                     k == 0, k == KC - 1)
                    last.then_inc(S["g"], 1)
                    if j > 0:
                        pe.wait_ge(S["bv"], nth("bv", b, j))
                    elif not is_first(b):
                        pe.wait_ge(S["bv"], nth("bv", b - 1, NJ))
                    for k in range(KC):
                        last = three(U_PS[:, 0:BW], xh[:, k, :], xl[:, k, :], wgu_hi[:, j, k, 1, :], wgu_lo[:, j, k, 1, :],
                                     k == 0, k == KC - 1)
                    last.then_inc(S["u"], 1)
                return f

            def T_(j):
                def f(b):
                    if j > 0:
                        pe.wait_ge(S["hl"], nth("hl", b, j))
                    else:
                        pe.wait_ge(S["xl"], nth("xl", b))
                    pe.wait_ge(S["h"], nth("h", b, j + 1))
                    for n in range(TC):
                        last = t.transpose(T_PS[:, n * P:(n + 1) * P], hv[:, n * P:(n + 1) * P], ident)
                    last.then_inc(S["T"], 1)
                return f

            def D_(j):
                def f(b):
                    if j == 0:
                        pe.wait_ge(S["eall"], nth("eall", b))
                    pe.wait_ge(S["hl"], nth("hl", b, j + 1))
                    for n in range(TC):
                        last = three(Y_PS[:, 0:D], hh[:, n, :], hl[:, n, :], wd_hi[:, j, n, :], wd_lo[:, j, n, :],
                                     j == 0 and n == 0, j == NJ - 1 and n == TC - 1)
                    last.then_inc(S["dn"], 1)
                return f

            schedule(pe, {"r3": r3, "r4": r4, "r6": r6, "r7": r7, "r8": r8, "r9": r9, "r11": r11, "r12": r12, "r13": r13,
                          "r15": r15, "r16": r16, "r17": r17, "r18": r18, "r19": r19,
                          **{f"mx{u}": mx(u) for u in range(8)}, "c": c, **{f"s{g}": s_(g) for g in range(NG)},
                          **{f"pv{g}": pv(g) for g in range(NG)}, "oT": oT_, "wo": wo_, "xT": xT, "lg": lg,
                          **{f"gu{j}": gu(j) for j in range(NJ)}, **{f"T{j}": T_(j) for j in range(NJ)},
                          **{f"D{j}": D_(j) for j in range(NJ)}})


def shape_constants(np):
    p = np.arange(P)
    c = np.zeros((P, CW), np.float32)
    c[:, 0:P] = np.eye(P)
    c[:, P:2 * P] = np.where(p[None, :] <= p[:, None], 0.0, -BIG)
    inv = (1.0 / np.float32(10000.0) ** (np.arange(0, DC, 2, dtype=np.float32) / np.float32(DC))).astype(np.float32)
    f = p.astype(np.float32)[:, None] * inv[None, :]
    cos, sin = np.concatenate([np.cos(f)] * 2, 1), np.concatenate([-np.sin(f), np.sin(f)], 1)
    scale = np.float32(1.0) / np.sqrt(np.float32(DC))
    at = 2 * P
    c[:, at:at + 2 * DC] = np.concatenate([cos * scale, cos], 1)
    c[:, at + 2 * DC:at + 4 * DC] = np.concatenate([sin * scale, sin], 1)
    at += 4 * DC
    c[:, at:at + NG] = (p[:, None] // HD) % NG == np.arange(NG)[None, :]
    c[:, at + NG:at + NG + HG] = p[:, None] % HG == np.arange(HG)[None, :]
    c[:, at + NG + HG:] = (p[:, None] % 32) // HG == np.arange(NG)[None, :]
    return c


def kernel(**inputs):
    import numpy as np
    import concourse.bacc as bacc
    from concourse import mybir as mb
    from concourse.bass_utils import run_bass_kernel_spmd as run

    a = {n: np.asarray(v) for n, v in inputs.items()}

    def cols(w):
        return w.T.reshape(KC, P, -1).transpose(1, 0, 2)

    wq, wkv = a["L0_attn_W_q_comp"].T, a["L0_attn_W_kv_comp"].T
    wk, wv = wkv[:, :DC], wkv[:, DC:]
    turn = np.concatenate([np.arange(DC // 2, DC), np.arange(DC // 2)])
    xq = a["L0_xattn_w_q"].reshape(NG, HG, HD, D).transpose(1, 0, 2, 3).reshape(D, D)
    arrays = {
        "x": a["x"],
        "ctxT": a["ctx_2048"].transpose(0, 2, 1).reshape(NB, KC, P, P).transpose(0, 2, 1, 3),
        "mask": a["mask_BxS2_if1"],
        "wgu": a["L0_ffn_gate_up_proj"].reshape(NJ, EJ, 2, NI, KC, P).transpose(5, 0, 4, 2, 1, 3).reshape(P, NJ, KC * 2 * BW),
        "wd": a["L0_ffn_down_proj"].transpose(0, 2, 1).reshape(NJ, TC, P, D).transpose(2, 0, 1, 3).reshape(P, NJ, TC * D),
        "gateT": cols(a["L0_ffn_gate_weight"]),
        "wtokv": a["L0_attn_W_to_kv"],
        "wcompT": a["L0_attn_W_compress"].T,
        "woutresT": a["L0_attn_W_out_res"].T,
        "wc2l": a["L0_attn_W_comp2lat"],
        "wqkv": np.concatenate([wq, wk, wq[:, turn], wk[:, turn], wv], 1),
        "gb": np.stack([a["L0_attn_ln_gamma"], a["L0_attn_ln_beta"]], 1),
        "bias2": np.broadcast_to(np.stack([a["L0_attn_b_out_res"], a["L0_xattn_b_o"]])[None], (P, 2, D)),
        "wq": cols(xq),
        "wkv": cols(np.concatenate([a["L0_xattn_w_k"], a["L0_xattn_w_v"]], 0)),
        "wo": cols(a["L0_xattn_w_o"]),
        "consts": shape_constants(np),
    }
    arrays = {n: np.ascontiguousarray(v) for n, v in arrays.items()}
    nc = bacc.Bacc("TRN2", target_bir_lowering=False, num_devices=1)
    args = {n: nc.dram_tensor(n + "_d", v.shape, mb.dt.from_np(v.dtype), kind="ExternalInput").ap() for n, v in arrays.items()}
    out = nc.dram_tensor("out_d", (NB, P, D), mb.dt.float32, kind="ExternalOutput").ap()
    decoder_kernel(nc, **args, out=out)
    r = run(nc, [{n + "_d": v for n, v in arrays.items()}], core_ids=[0])
    return r.results[0]["out_d"]
```

```python
import concourse.bass as bass
from concourse import mybir
from contextlib import ExitStack

NB, P, D = 16, 128, 256
KC = D // P
NE, NI = 32, 96
NJ, EJ = 8, 4
BW = EJ * NI
PW = 2 * BW
TC = BW // P
NG, HG, HD = 8, 4, 8
GD = NG * HD
DL, DC = 64, 32
CW = 2 * P + 4 * DC + NG + HG + NG
BIG = 1e30
EPS = 1e-5
NPT = 4
KEEP = 0.8


ORDER = """
gate2 gate3 gu0 ab0 gate4 mx0 mx1 gu1 ab1 r1 mx2 mx3 T0 gu2 r2 mx4 mx5 ab2 D0 r3 T1 mx6 r4 mx7 gu3 r5 c D1 r6 s0 ab3 T2 s1 r7 s2 gu4 s3 r8 D2 T3 r9 pv0 ab4 r10 s4 D3 s5 vt0 T4 r11 s6 s7 r12 gu5 ab5 r13 pv1 r14 D4 vt1 ab6 T5 r15 oT gu6 wo r16 D5 T6 ab7 r17 gu7 n3 D6 r18 xT T7 r19 lg D7 res gate1 y
""".split()
EXPERTS = {f"{s}{j}" for s in ("gu", "ab", "T", "D") for j in range(NJ)} | {"gate2", "gate3", "gate4", "y"}
FRONT = [s for s in ORDER if s[0] == "r" and s[1:].isdigit()]
CROSS = [s for s in ORDER if s not in FRONT and s not in EXPERTS]

READ = {**{f"mx{u}": ("rmax", u + 1) for u in range(8)}, "c": ("Q3c", 1), **{f"s{g}": ("e", g + 1) for g in range(NG)},
        **{f"vt{n}": ("on", n + 1) for n in range(2)}, "oT": ("oT2_sb", 1), "wo": ("x2", 1), "xT": ("xl", 1), "lg": ("eall", 1)}
USES = [s for s in CROSS if s in READ]


def decoder_kernel(nc, x, ctxT, mask, wgu, wd, gateT, wtokv, wcompT, woutresT, wc2l, wqkv, gb, bias2,
                   wq, wkv, wo, consts, out):
    f32, f32r, bf16, i32 = mybir.dt.float32, mybir.dt.float32r, mybir.dt.bfloat16, mybir.dt.int32
    ALU, ACT, AX = mybir.AluOpType, mybir.ActivationFunctionType, mybir.AxisListType.X

    with ExitStack() as ctx:
        def sb(name, shape, dt=f32):
            return ctx.enter_context(nc.sbuf_tensor(name, shape, dt))

        scalars, used = sb("scalars", [P, 32]), iter(range(32))

        def one():
            n = next(used)
            return scalars[:, n:n + 1]

        wgu_hi, wgu_lo = (sb(n, [P, NJ, KC, 2, BW], f32r) for n in ("wgu_hi", "wgu_lo"))
        wd_hi, wd_lo = (sb(n, [P, NJ, TC, D], f32r) for n in ("wd_hi", "wd_lo"))
        gate_f = sb("gate_f", [P, KC, NE])
        gate_hi, gate_lo = (sb(n, [P, KC, NE], f32r) for n in ("gate_hi", "gate_lo"))
        con = sb("con", [P, CW])
        ident = con[:, 0:P]
        causal = con[:, P:2 * P]
        at0 = 2 * P
        cos = con[:, at0:at0 + 2 * DC]
        sin = con[:, at0 + 2 * DC:at0 + 4 * DC]
        at0 += 4 * DC
        own8 = con[:, at0:at0 + NG]
        own4 = con[:, at0 + NG:at0 + NG + HG]
        sel8 = con[:, at0 + NG + HG:at0 + 2 * NG + HG]
        ident16, causal16 = sb("ident16", [P, P], bf16), sb("causal16", [P, P], bf16)
        half, eps, zero, idle = (one() for _ in range(4))
        wc = sb("wc", [P, KC, DC])
        wback = sb("wback", [DC, D])
        wqkv_sb = sb("wqkv_sb", [DC, 5 * DC])
        gb_sb = sb("gb_sb", [DC, 2])
        bias_sb = sb("bias_sb", [P, 2, D])
        wq_sb, wo_sb = sb("wq_sb", [P, KC, D]), sb("wo_sb", [P, KC, D])
        wkv_sb = sb("wkv_sb", [P, KC, 2 * GD])
        xin, x1, x1b, xn, xnT = (sb(n, [P, D]) for n in ("xin", "x1", "x1b", "xn", "xnT"))
        x1n, x1nT = xn, xnT
        ctx_sb = sb("ctx_sb", [P, KC, P])
        mrow, mcol = sb("mrow", [P, P], i32), sb("mcol", [P, 1], i32)
        st = {n: sb("st_" + n, [P, 6]) for n in ("ln1", "lnc", "ln2", "ln3")}
        mv = {n: sb("mv_" + n, [P, 2]) for n in ("ln1", "lnc", "ln2", "ln3")}
        veps = {n: one() for n in ("ln1", "lnc", "ln2", "ln3")}
        rstd = {n: one() for n in ("ln1", "lnc", "ln2", "ln3")}
        chat, chT = sb("chat", [P, DC]), sb("chT", [DC, P])
        rope_s, qk = (sb(n, [P, 2 * DC]) for n in ("rope_s", "qk"))
        v_sb, qkT = sb("v_sb", [P, DC]), sb("qkT", [DC, 2, P])
        nmax, den, rden = (one() for _ in range(3))
        prob, probT, oT_sb = sb("prob", [P, P]), sb("probT", [P, P]), sb("oT_sb", [DC, P])
        qN = sb("qN", [P, HG, 2, GD], f32r)
        Q2 = sb("Q2", [P, HG, P], f32r)
        Q3 = sb("Q3", [96, HG, P], f32r)
        kN = sb("kN", [P, 3, GD], f32r)
        kloT = prob[0:GD, :]
        KA = sb("KA", [P, NG, P], f32r)
        KB = sb("KB", [96, NG, P], f32r)
        va = sb("va", [P, NG * (HD + 1) + 32])
        va_g = va[:, 0:NG * (HD + 1)].rearrange("p (g d) -> p g d", g=NG)
        padrow = mrow[:, :].bitcast(f32)
        maskn = sb("maskn", [P, P], bf16)
        padcol = one()
        negc = sb("negc", [P, P])
        PT = sb("PT", [P, NPT, HG, P])
        rdx = sb("rdx", [P, NG * HG])
        o_nat, oT2, x2, x2r = (sb(n, [P, D]) for n in ("o_nat", "oT2", "x2", "x2r"))
        x2n = o_nat
        xh, xl = sb("xh", [P, KC, P], f32r), sb("xl", [P, KC, P], f32r)
        nlmax, eall, e8 = one(), sb("eall", [P, NE]), sb("e8", [P, 8])
        tot, rtot, ksum, rk, thr = (one() for _ in range(5))
        cum = [sb(f"cum{n}", [P, 16]) for n in range(4)]
        kept, out8 = sb("kept", [P, 8]), sb("out8", [P, 8])
        ehalf, cm, ce = (sb(n, [P, NE]) for n in ("ehalf", "cm", "ce"))
        work = sb("work", [P, 4, BW])
        th, av, bv, hv = (work[:, n, :] for n in range(4))
        stage = work[:, :, :].rearrange("p (s a) n -> p s (a n)", s=2)
        hh, hl = sb("hh", [P, TC, P], f32r), sb("hl", [P, TC, P], f32r)
        y = sb("y", [P, D])
        l_tokv, l_outres = y[0:DL, :], x2r[0:DL, :]
        l_comp, l_c2l = oT2[0:DL, 0:DC], oT2[0:DL, DC:2 * DC]
        bank = [ctx.enter_context(nc.psum_tensor(f"bank{n}", [P, 512], f32)) for n in range(8)]
        G_PS, U_PS, T_PS, Y_PS, R_PS, V_PS = bank[0:6]
        RING = bank[6:8]

        def ring_bank(use):
            return RING[USES.index(use) % 2]

        def slot(g):
            return g if g < NPT else (g + 1) % NPT

        PER = dict(mx=8, rmax=8, s=8, e=8, pm=8, pv=2, vc=2, vt=2, rdx=2, on=2, g=8, u=8, th=8, av=8, bv=8, h=8, T=8, hh=8, hl=8, dn=8)
        names = ("x_in ctx_in m_in w_small w_hi w_lo setup_v setup_g setup_p setup_a "
                 "st1 mv1 ve1 rs1 xb xn xnT xnT_sb c stc mvc vec rsc chat chatT chT qkv rc rsn qk v_sb qkT qkT_sb "
                 "ss smax p rden pT pT_sb oT oT_sb o1 x1 st2 mv2 ve2 rs2 x1b x1n x1nT x1nT_sb q qh ql qT Q2 Q3t "
                 "kv kh klo va kT kloT KA KB pr pr2 pc "
                 "mx rmax cT Q3c s e pm pv vc vt rdx on oT2 oT2_sb wo x2 st3 mv3 ve3 rs3 x2n "
                 "x2r xT xh xl lg nlmax eall eh e8 tot rtot cu0 cu1 cu2 cu3 ksum out8a out8b thr rk cm ce "
                 "g u th av bv h T hh hl dn y out").split()
        S = {n: ctx.enter_context(nc.semaphore("s_" + n)) for n in names}
        S["w_in"] = [ctx.enter_context(nc.semaphore(f"s_w_in{n}")) for n in range(2)]

        def nth(name, b, k=1):
            return b * PER.get(name, 1) + k

        block = ctx.enter_context(nc.Block())

        def piece_of(gu, dn, j, n):
            return gu[:, j, n, :, :].rearrange("p g n -> p (g n)") if n < KC else dn[:, j, :, :].rearrange("p t n -> p (t n)")

        def is_first(b):
            return isinstance(b, int) and b == 0

        def schedule(eng, steps):
            def iteration(i, front, cross):
                for s in ORDER:
                    if s in FRONT:
                        if front and s in steps:
                            steps[s](i + 2)
                    elif s in CROSS:
                        if cross and s in steps:
                            steps[s](i + 1)
                    elif s in steps:
                        steps[s](i)

            for n, s in enumerate(FRONT):
                if s in steps:
                    steps[s](0)
                if n % 3 == 2 and "split" in steps and n // 3 < 3:
                    steps["split"](n // 3)
            for n in range(19):
                s = FRONT[n]
                for c in CROSS[n * len(CROSS) // 19:(n + 1) * len(CROSS) // 19]:
                    if c in steps:
                        steps[c](0)
                if s in steps:
                    steps[s](1)
                if n % 3 == 2 and "split" in steps and 3 + n // 3 < NJ:
                    steps["split"](3 + n // 3)
            iteration(0, True, True)
            with eng.Fori(1, NB - 2) as i:
                iteration(i, True, True)
            iteration(NB - 2, False, True)
            iteration(NB - 1, False, False)

        def row(t, b):
            if isinstance(b, int):
                return t[b]
            return t[bass.ds(b, 1)].squeeze(0)

        @block.sync
        def _(sp):
            for dst, src in ((con[:, :], consts), (l_tokv, wtokv), (l_outres, woutresT), (l_comp, wcompT),
                             (l_c2l, wc2l), (wqkv_sb[:, :], wqkv), (gb_sb[:, :], gb), (bias_sb[:, :, :], bias2),
                             (wq_sb[:, :, :], wq), (wkv_sb[:, :, :], wkv), (wo_sb[:, :, :], wo), (gate_f[:, :, :], gateT)):
                sp.dma_start(dst, src).then_inc(S["w_small"], 16)

            def load_batch(b):
                if not is_first(b):
                    sp.wait_ge(S["x1"], nth("x1", b - 1))
                sp.dma_start(xin[:, :], row(x, b)).then_inc(S["x_in"], 16)
                if not is_first(b):
                    sp.wait_ge(S["kv"], nth("kv", b - 1))
                    sp.wait_ge(S["pr2"], nth("pr2", b - 1))
                    sp.wait_ge(S["pc"], nth("pc", b - 1))
                sp.dma_start(ctx_sb[:, :, :], row(ctxT, b)).then_inc(S["ctx_in"], 16)
                sp.dma_start(mrow[:, :], row(mask, b).partition_broadcast(P)).then_inc(S["m_in"], 16)
                sp.dma_start(mcol[:, :], row(mask, b).rearrange("(p o) -> p o", o=1)).then_inc(S["m_in"], 16)

            def load_split(j):
                for n in range(3):
                    piece = 3 * j + n
                    if piece >= 2:
                        sp.wait_ge(S["w_lo"], piece - 1)
                    src = wgu[:, j, n * PW:(n + 1) * PW] if n < KC else wd[:, j, :]
                    sp.dma_start(stage[:, piece % 2, :], src).then_inc(S["w_in"][piece % 2], 16)

            def store(b):
                sp.wait_ge(S["y"], nth("y", b))
                sp.dma_start(row(out, b), y[:, :]).then_inc(S["out"], 16)

            def r1(b):
                if is_first(b):
                    load_batch(b)

            def mx0(b):
                if not isinstance(b, int) or b + 1 < NB:
                    load_batch(b + 1)

            schedule(sp, {"r1": r1, "mx0": mx0, "split": load_split, "y": store})
            sp.wait_ge(S["out"], 16 * NB)

        @block.gpsimd
        def _(pool):
            gp = nc.gpsimd

            def landed():
                gp.tensor_tensor(idle[:, :], zero[:, :], zero[:, :], ALU.add)
            gp.memset(half[:, :], -0.5).then_inc(S["setup_g"], 1)
            gp.memset(eps[:, :], EPS).then_inc(S["setup_g"], 1)
            gp.memset(zero[:, :], 0.0).then_inc(S["setup_g"], 1)
            gp.memset(negc[:, :], 0.0).then_inc(S["setup_g"], 1)
            gp.memset(va[:, NG * (HD + 1):], 0.0).then_inc(S["setup_g"], 1)
            gp.memset(va_g[:, :, HD:HD + 1], 1.0).then_inc(S["setup_g"], 1)
            for c in cum:
                gp.memset(c[:, 0:8], 0.0).then_inc(S["setup_g"], 1)
            pool.wait_ge(S["w_small"], 12 * 16)
            gp.tensor_copy(ident16[:, :], ident).then_inc(S["setup_g"], 1)
            gp.tensor_copy(causal16[:, :], causal).then_inc(S["setup_g"], 1)
            pool.wait_ge(S["setup_g"], 3)

            def inv_std(ln, sm, sv, sr, b):
                pool.wait_ge(S[sm], nth(sm, b))
                gp.tensor_tensor(veps[ln][:, :], mv[ln][:, 1:2], eps[:, :], ALU.add).then_inc(S[sv], 1)
                pool.wait_ge(S[sv], nth(sv, b))
                gp.tensor_tensor(rstd[ln][:, :], veps[ln][:, :], half[:, :], ALU.pow).then_inc(S[sr], 1)

            def r1(b):
                inv_std("ln1", "mv1", "ve1", "rs1", b)

            def r2(b):
                pool.wait_ge(S["xn"], nth("xn", b))
                gp.tensor_tensor(xin[:, :], xin[:, :], bias_sb[:, 0, :], ALU.add).then_inc(S["xb"], 1)

            def r4(b):
                inv_std("lnc", "mvc", "vec", "rsc", b)

            def r13(b):
                inv_std("ln2", "mv2", "ve2", "rs2", b)

            def r17(b):
                pool.wait_ge(S["x1"], nth("x1", b))
                if not is_first(b):
                    pool.wait_ge(S["x2"], nth("x2", b - 1))
                gp.tensor_tensor(x1b[:, :], x1[:, :], bias_sb[:, 1, :], ALU.add).then_inc(S["x1b"], 1)
                pool.wait_ge(S["Q2"], nth("Q2", b))
                gp.tensor_tensor(Q3[0:GD, :, :], Q2[0:GD, :, :].bitcast(f32), zero[0:GD, :].unsqueeze(2).to_broadcast([GD, HG, P]),
                                 ALU.add).then_inc(S["Q3t"], 1)

            def r18(b):
                if not is_first(b):
                    pool.wait_ge(S["mx"], nth("mx", b - 1, 8))
                pool.wait_ge(S["pr"], nth("pr", b))
                gp.tensor_tensor(maskn[:, :], padrow, causal, ALU.add).then_inc(S["pr2"], 1)

            def r19(b):
                pool.wait_ge(S["kloT"], nth("kloT", b))
                if not is_first(b):
                    pool.wait_ge(S["s"], nth("s", b - 1, 8))
                gp.tensor_tensor(KB[0:GD, :, :], kloT.unsqueeze(1).to_broadcast([GD, NG, P]),
                                 own8[0:GD, :].unsqueeze(2).to_broadcast([GD, NG, P]), ALU.mult).then_inc(S["KB"], 1)

            def s_(g):
                def f(b):
                    if g > 0:
                        pool.wait_ge(S["pm"], nth("pm", b, g))
                    elif not is_first(b):
                        pool.wait_ge(S["pm"], nth("pm", b - 1, NG))
                    pool.wait_ge(S["e"], nth("e", b, g + 1))
                    landed()
                    gp.affine_select(out=PT[:, slot(g), :, :], in_=PT[:, slot(g), :, :], compare_op=ALU.is_ge, fill=0.0, base=0,
                                     pattern=[[0, HG], [1, P]], channel_multiplier=-1).then_inc(S["pm"], 1)
                return f

            def wo_(b):
                inv_std("ln3", "mv3", "ve3", "rs3", b)

            def res(b):
                pool.wait_ge(S["x2"], nth("x2", b))
                if not is_first(b):
                    pool.wait_ge(S["y"], nth("y", b - 1))
                gp.tensor_tensor(x2r[:, :], x2[:, :], zero[:, :].to_broadcast([P, D]), ALU.add).then_inc(S["x2r"], 1)

            def ab(j):
                def f(b):
                    pool.wait_ge(S["bv"], nth("bv", b, j + 1))
                    pool.wait_ge(S["ce"], nth("ce", b))
                    if j > 0:
                        pool.wait_ge(S["T"], nth("T", b, j))
                    elif not is_first(b):
                        pool.wait_ge(S["T"], nth("T", b - 1, NJ))
                    gp.tensor_tensor(hv.rearrange("p (e i) -> p e i", e=EJ), bv.rearrange("p (e i) -> p e i", e=EJ),
                                     ce[:, EJ * j:EJ * j + EJ].unsqueeze(2).to_broadcast([P, EJ, NI]), ALU.mult).then_inc(S["h"], 1)
                return f

            schedule(pool, {"r1": r1, "r2": r2, "r4": r4, "r13": r13, "r17": r17, "r18": r18, "r19": r19, "wo": wo_, "res": res,
                            **{f"s{g}": s_(g) for g in range(NG)}, **{f"ab{j}": ab(j) for j in range(NJ)}})

        @block.scalar
        def _(act):
            ac = nc.scalar

            def copy(o, i):
                return ac.activation(o, i, ACT.Copy)

            act.wait_ge(S["setup_p"], 2)
            copy(wc[:, :, :], R_PS[:, 0:KC * DC].rearrange("p (k c) -> p k c", k=KC)).then_inc(S["setup_a"], 1)
            copy(wback[:, :], R_PS[0:DC, 128:128 + D]).then_inc(S["setup_a"], 1)
            copy(gate_hi[:, :, :], gate_f[:, :, :]).then_inc(S["setup_a"], 1)
            copy(KB[GD:96, :, :], sel8[GD:96, :].unsqueeze(2).to_broadcast([32, NG, P])).then_inc(S["setup_a"], 1)

            def split(j):
                for n in range(3):
                    piece = 3 * j + n
                    act.wait_ge(S["w_in"][piece % 2], 16 * (piece // 2 + 1))
                    copy(piece_of(wgu_hi, wd_hi, j, n), stage[:, piece % 2, :]).then_inc(S["w_hi"], 1)

            def r3(b):
                act.wait_ge(S["xnT"], nth("xnT", b))
                copy(xnT[:, :], R_PS[:, 0:D]).then_inc(S["xnT_sb"], 1)

            def r8(b):
                act.wait_ge(S["qkT"], nth("qkT", b))
                copy(qkT[:, :, :], R_PS[0:DC, 0:2 * P].rearrange("p (a n) -> p a n", a=2)).then_inc(S["qkT_sb"], 1)

            def r10(b):
                act.wait_ge(S["smax"], nth("smax", b))
                ac.activation(prob[:, :], R_PS[:, 0:P], ACT.Exp, bias=nmax[:, :], accum_out=den[:, :]).then_inc(S["p"], 1)

            def r11(b):
                act.wait_ge(S["pT"], nth("pT", b))
                copy(probT[:, :], R_PS[:, 0:P]).then_inc(S["pT_sb"], 1)

            def r12(b):
                act.wait_ge(S["oT"], nth("oT", b))
                copy(oT_sb[:, :], R_PS[0:DC, 0:P]).then_inc(S["oT_sb"], 1)

            def r15(b):
                act.wait_ge(S["x1nT"], nth("x1nT", b))
                copy(x1nT[:, :], R_PS[:, 0:D]).then_inc(S["x1nT_sb"], 1)

            def r16(b):
                act.wait_ge(S["q"], nth("q", b))
                copy(qN[:, :, 0, :], R_PS[:, 0:D].rearrange("p (h c) -> p h c", h=HG)).then_inc(S["qh"], 1)

            def r17(b):
                act.wait_ge(S["qT"], nth("qT", b))
                if not is_first(b):
                    act.wait_ge(S["s"], nth("s", b - 1, 8))
                copy(Q2[:, :, :], R_PS[:, :].rearrange("p (h n) -> p h n", h=HG)).then_inc(S["Q2"], 1)

            def r18(b):
                act.wait_ge(S["kv"], nth("kv", b))
                copy(kN[:, 0:2, :], R_PS[:, 0:GD].unsqueeze(1).to_broadcast([P, 2, GD])).then_inc(S["kh"], 1)
                if is_first(b):
                    act.wait_ge(S["setup_g"], 6)
                else:
                    act.wait_ge(S["pv"], nth("pv", b - 1, 2))
                copy(va_g[:, :, 0:HD], R_PS[:, GD:2 * GD].rearrange("p (g d) -> p g d", g=NG)).then_inc(S["va"], 1)

            def r19(b):
                act.wait_ge(S["kT"], nth("kT", b))
                if not is_first(b):
                    act.wait_ge(S["KB"], nth("KB", b - 1))
                copy(kloT, R_PS[0:GD, P:2 * P]).then_inc(S["kloT"], 1)

            def s_(g):
                def f(b):
                    act.wait_ge(S["s"], nth("s", b, g + 1))
                    if g == 0:
                        act.wait_ge(S["pc"], nth("pc", b))
                    if g == NPT:
                        act.wait_ge(S["pv"], nth("pv", b))
                    if g == NG - 1:
                        act.wait_ge(S["vt"], nth("vt", b))
                    ac.activation(PT[:, slot(g), :, :].rearrange("p h n -> p (h n)"), ring_bank(f"s{g}")[:, :], ACT.Exp,
                                  bias=padcol[:, :], scale=float(HD) ** -0.5).then_inc(S["e"], 1)
                return f

            def pv(n):
                def f(b):
                    act.wait_ge(S["pv"], nth("pv", b, n + 1))
                    copy(PT[:, n, :, :].rearrange("p h n -> p (h n)"), V_PS[:, :]).then_inc(S["vc"], 1)
                return f

            def oT_(b):
                act.wait_ge(S["oT2"], nth("oT2", b))
                copy(oT2[:, :], ring_bank("oT")[:, 0:D]).then_inc(S["oT2_sb"], 1)

            def xT(b):
                act.wait_ge(S["xT"], nth("xT", b))
                if not is_first(b):
                    act.wait_ge(S["u"], nth("u", b - 1, NJ))
                copy(xh[:, :, :], ring_bank("xT")[:, 0:D].rearrange("p (k n) -> p k n", k=KC)).then_inc(S["xh"], 1)

            def gate1(b):
                act.wait_ge(S["nlmax"], nth("nlmax", b))
                ac.activation(eall[:, :], ring_bank("lg")[:, 0:NE], ACT.Exp, bias=nlmax[:, :]).then_inc(S["eall"], 1)

            def gu(j):
                def f(b):
                    act.wait_ge(S["g"], nth("g", b, j + 1))
                    ac.activation(th, G_PS[:, 0:BW], ACT.Tanh, scale=0.5).then_inc(S["th"], 1)
                return f

            def T_(j):
                def f(b):
                    act.wait_ge(S["T"], nth("T", b, j + 1))
                    copy(hh[:, :, :], T_PS[:, 0:BW].rearrange("p (t n) -> p t n", t=TC)).then_inc(S["hh"], 1)
                return f

            schedule(act, {"split": split, "r3": r3, "r8": r8, "r10": r10, "r11": r11, "r12": r12, "r15": r15,
                           "r16": r16, "r17": r17, "r18": r18, "r19": r19, "oT": oT_, "xT": xT, "gate1": gate1, "pv0": pv(0), "pv1": pv(1),
                           **{f"s{g}": s_(g) for g in range(NG)},
                           **{f"gu{j}": gu(j) for j in range(NJ)}, **{f"T{j}": T_(j) for j in range(NJ)}})

        @block.vector
        def _(dve):
            v = nc.vector
            dve.wait_ge(S["w_small"], 12 * 16)
            v.tensor_tensor(l_outres, l_outres, l_tokv, ALU.add).then_inc(S["setup_v"], 1)
            dve.wait_ge(S["setup_a"], 3)
            v.tensor_tensor(gate_lo[:, :, :], gate_f[:, :, :], gate_hi[:, :, :].bitcast(f32), ALU.subtract).then_inc(S["setup_v"], 1)

            def stats(ln, src, ss, sm, b):
                v.bn_stats(st[ln][:, :], src).then_inc(S[ss], 1)
                dve.drain()
                v.bn_aggr(mv[ln][:, :], st[ln][:, :]).then_inc(S[sm], 1)

            def normal(ln, o, src):
                return v.tensor_scalar(o, src, mv[ln][:, 0:1], rstd[ln][:, :], ALU.subtract, ALU.mult)

            def split(j):
                for n in range(3):
                    piece = 3 * j + n
                    dve.wait_ge(S["w_hi"], piece + 1)
                    v.tensor_tensor(piece_of(wgu_lo, wd_lo, j, n), stage[:, piece % 2, :],
                                    piece_of(wgu_hi, wd_hi, j, n).bitcast(f32), ALU.subtract).then_inc(S["w_lo"], 1)

            def r1(b):
                dve.wait_ge(S["x_in"], 16 * b + 16)
                stats("ln1", xin[:, :], "st1", "mv1", b)

            def r2(b):
                dve.wait_ge(S["rs1"], nth("rs1", b))
                normal("ln1", xn[:, :], xin[:, :]).then_inc(S["xn"], 1)

            def r4(b):
                dve.wait_ge(S["c"], nth("c", b))
                stats("lnc", R_PS[:, 0:DC], "stc", "mvc", b)

            def r5(b):
                dve.wait_ge(S["rsc"], nth("rsc", b))
                normal("lnc", chat[:, :], R_PS[:, 0:DC]).then_inc(S["chat"], 1)

            def r6(b):
                dve.wait_ge(S["chatT"], nth("chatT", b))
                v.tensor_scalar(chT[:, :], R_PS[0:DC, 0:P], gb_sb[:, 0:1], gb_sb[:, 1:2], ALU.mult, ALU.add).then_inc(S["chT"], 1)

            def r7(b):
                dve.wait_ge(S["qkv"], nth("qkv", b))
                v.tensor_tensor(qk[:, :], R_PS[:, 0:2 * DC], cos, ALU.mult).then_inc(S["rc"], 1)
                v.tensor_tensor(rope_s[:, :], R_PS[:, 2 * DC:4 * DC], sin, ALU.mult).then_inc(S["rsn"], 1)
                v.tensor_copy(v_sb[:, :], R_PS[:, 4 * DC:5 * DC]).then_inc(S["v_sb"], 1)
                dve.wait_ge(S["rc"], nth("rc", b))
                dve.wait_ge(S["rsn"], nth("rsn", b))
                v.tensor_tensor(qk[:, :], qk[:, :], rope_s[:, :], ALU.add).then_inc(S["qk"], 1)

            def r9(b):
                dve.wait_ge(S["ss"], nth("ss", b))
                v.tensor_reduce(nmax[:, :], R_PS[:, 0:P], AX, ALU.max, negate=True).then_inc(S["smax"], 1)

            def r10(b):
                dve.wait_ge(S["p"], nth("p", b))
                v.reciprocal(rden[:, :], den[:, :]).then_inc(S["rden"], 1)

            def r13(b):
                dve.wait_ge(S["o1"], nth("o1", b))
                dve.wait_ge(S["rden"], nth("rden", b))
                dve.wait_ge(S["xb"], nth("xb", b))
                if not is_first(b):
                    dve.wait_ge(S["x1b"], nth("x1b", b - 1))
                v.scalar_tensor_tensor(x1[:, :], R_PS[:, 0:D], rden[:, :], xin[:, :], ALU.mult, ALU.add).then_inc(S["x1"], 1)
                dve.wait_ge(S["x1"], nth("x1", b))
                stats("ln2", x1[:, :], "st2", "mv2", b)

            def r14(b):
                dve.wait_ge(S["rs2"], nth("rs2", b))
                normal("ln2", x1n[:, :], x1[:, :]).then_inc(S["x1n"], 1)

            def r16(b):
                dve.wait_ge(S["qh"], nth("qh", b))
                v.tensor_tensor(qN[:, :, 1, :], R_PS[:, 0:D].rearrange("p (h c) -> p h c", h=HG),
                                qN[:, :, 0, :].bitcast(f32), ALU.subtract).then_inc(S["ql"], 1)

            def r18(b):
                dve.wait_ge(S["m_in"], 32 * b + 32)
                v.tensor_scalar(padrow, mrow[:, :], 0.0, -BIG, ALU.is_equal, ALU.mult).then_inc(S["pr"], 1)
                if not is_first(b):
                    dve.wait_ge(S["e"], nth("e", b - 1, 8))
                v.tensor_scalar(padcol[:, :], mcol[:, :], 0.0, -BIG, ALU.is_equal, ALU.mult).then_inc(S["pc"], 1)
                dve.wait_ge(S["va"], nth("va", b))
                v.tensor_tensor(kN[:, 2, :], R_PS[:, 0:GD], kN[:, 0, :].bitcast(f32), ALU.subtract).then_inc(S["klo"], 1)

            def r19(b):
                dve.wait_ge(S["kloT"], nth("kloT", b))
                if not is_first(b):
                    dve.wait_ge(S["s"], nth("s", b - 1, 8))
                v.tensor_tensor(KA[:, :, :], R_PS[:, 0:P].unsqueeze(1).to_broadcast([P, NG, P]),
                                own8.unsqueeze(2).to_broadcast([P, NG, P]), ALU.mult).then_inc(S["KA"], 1)

            def mx(u):
                hg, hf = u % HG, u // HG
                def f(b):
                    if u == 0 and is_first(b):
                        dve.wait_ge(S["setup_g"], 4)
                    dve.wait_ge(S["mx"], nth("mx", b, u + 1))
                    at = GD + 16 * hf + hg
                    v.tensor_reduce(negc[:, at:at + 13:HG], ring_bank(f"mx{u}")[:, :].rearrange("p (g m) -> p g m", g=HG), AX, ALU.max,
                                    negate=True).then_inc(S["rmax"], 1)
                return f

            def c(b):
                dve.wait_ge(S["cT"], nth("cT", b))
                v.tensor_tensor(Q3[GD:96, :, :], ring_bank("c")[GD:96, 0:P].unsqueeze(1).to_broadcast([32, HG, P]),
                                own4[GD:96, :].unsqueeze(2).to_broadcast([32, HG, P]), ALU.mult).then_inc(S["Q3c"], 1)

            def on(n):
                def f(b):
                    heads = ring_bank(f"vt{n}")[:, :].rearrange("p (h g d) -> p g h d", h=HG, g=NPT)
                    rd = rdx[:, :].rearrange("p (n g h) -> p n g h", n=2, g=NPT)[:, n, :, :].unsqueeze(3)
                    dve.wait_ge(S["vt"], nth("vt", b, n + 1))
                    v.reciprocal(rd, heads[:, :, :, HD:HD + 1]).then_inc(S["rdx"], 1)
                    dve.wait_ge(S["rdx"], nth("rdx", b, n + 1))
                    v.tensor_tensor(o_nat[:, n * P:(n + 1) * P].rearrange("p (g h d) -> p g h d", g=NPT, h=HG), heads[:, :, :, 0:HD],
                                    rd.to_broadcast([P, NPT, HG, HD]), ALU.mult).then_inc(S["on"], 1)
                return f

            def wo_(b):
                dve.wait_ge(S["wo"], nth("wo", b))
                dve.wait_ge(S["x1b"], nth("x1b", b))
                if not is_first(b):
                    dve.wait_ge(S["x2r"], nth("x2r", b - 1))
                v.tensor_tensor(x2[:, :], ring_bank("wo")[:, 0:D], x1b[:, :], ALU.add).then_inc(S["x2"], 1)
                dve.wait_ge(S["x2"], nth("x2", b))
                stats("ln3", x2[:, :], "st3", "mv3", b)

            def n3(b):
                dve.wait_ge(S["rs3"], nth("rs3", b))
                normal("ln3", x2n[:, :], x2[:, :]).then_inc(S["x2n"], 1)

            def xT(b):
                dve.wait_ge(S["xh"], nth("xh", b))
                v.tensor_tensor(xl[:, :, :], ring_bank("xT")[:, 0:D].rearrange("p (k n) -> p k n", k=KC), xh[:, :, :].bitcast(f32),
                                ALU.subtract).then_inc(S["xl"], 1)

            def gate1(b):
                dve.wait_ge(S["lg"], nth("lg", b))
                v.tensor_reduce(nlmax[:, :], ring_bank("lg")[:, 0:NE], AX, ALU.max, negate=True).then_inc(S["nlmax"], 1)

            def gate2(b):
                if is_first(b):
                    dve.wait_ge(S["setup_g"], 10)
                dve.wait_ge(S["eall"], nth("eall", b))
                v.tensor_scalar(ehalf[:, :], eall[:, :], 0.5, None, ALU.mult).then_inc(S["eh"], 1)
                v.max(e8[:, :], eall[:, :]).then_inc(S["e8"], 1)
                dve.wait_ge(S["e8"], nth("e8", b))
                v.reduce_sum(tot[:, :], e8[:, :], AX).then_inc(S["tot"], 1)
                dve.wait_ge(S["tot"], nth("tot", b))
                v.reciprocal(rtot[:, :], tot[:, :]).then_inc(S["rtot"], 1)
                dve.wait_ge(S["rtot"], nth("rtot", b))
                v.tensor_scalar(cum[0][:, 8:16], e8[:, :], rtot[:, :], None, ALU.mult).then_inc(S["cu0"], 1)

            def gate3(b):
                for n, by in enumerate((1, 2, 4)):
                    dve.wait_ge(S[f"cu{n}"], nth(f"cu{n}", b))
                    v.tensor_tensor(cum[n + 1][:, 8:16], cum[n][:, 8:16], cum[n][:, 8 - by:16 - by], ALU.add).then_inc(S[f"cu{n + 1}"], 1)
                dve.wait_ge(S["cu3"], nth("cu3", b))
                v.scalar_tensor_tensor(kept[:, :], cum[3][:, 7:15], KEEP, e8[:, :], ALU.is_lt, ALU.mult,
                                       accum_out=ksum[:, :]).then_inc(S["ksum"], 1)
                v.tensor_scalar(out8[:, :], cum[3][:, 7:15], KEEP, 4.0, ALU.is_ge, ALU.mult).then_inc(S["out8a"], 1)

            def gate4(b):
                dve.wait_ge(S["out8a"], nth("out8a", b))
                v.tensor_tensor(out8[:, :], out8[:, :], e8[:, :], ALU.add).then_inc(S["out8b"], 1)
                dve.wait_ge(S["out8b"], nth("out8b", b))
                v.tensor_reduce(thr[:, :], out8[:, :], AX, ALU.min).then_inc(S["thr"], 1)
                dve.wait_ge(S["ksum"], nth("ksum", b))
                v.reciprocal(rk[:, :], ksum[:, :]).then_inc(S["rk"], 1)
                dve.wait_ge(S["thr"], nth("thr", b))
                dve.wait_ge(S["eh"], nth("eh", b))
                v.scalar_tensor_tensor(cm[:, :], eall[:, :], thr[:, :], ehalf[:, :], ALU.is_ge, ALU.mult).then_inc(S["cm"], 1)
                dve.wait_ge(S["cm"], nth("cm", b))
                dve.wait_ge(S["rk"], nth("rk", b))
                if not is_first(b):
                    dve.wait_ge(S["h"], nth("h", b - 1, NJ))
                v.tensor_scalar(ce[:, :], cm[:, :], rk[:, :], None, ALU.mult).then_inc(S["ce"], 1)

            def ab(j):
                def f(b):
                    dve.wait_ge(S["th"], nth("th", b, j + 1))
                    if j > 0:
                        dve.wait_ge(S["bv"], nth("bv", b, j))
                    elif not is_first(b):
                        dve.wait_ge(S["bv"], nth("bv", b - 1, NJ))
                    v.scalar_tensor_tensor(av, th, 1.0, G_PS[:, 0:BW], ALU.add, ALU.mult).then_inc(S["av"], 1)
                    dve.wait_ge(S["av"], nth("av", b, j + 1))
                    dve.wait_ge(S["u"], nth("u", b, j + 1))
                    if j > 0:
                        dve.wait_ge(S["h"], nth("h", b, j))
                    elif not is_first(b):
                        dve.wait_ge(S["h"], nth("h", b - 1, NJ))
                    v.tensor_tensor(bv, av, U_PS[:, 0:BW], ALU.mult).then_inc(S["bv"], 1)
                return f

            def T_(j):
                def f(b):
                    dve.wait_ge(S["hh"], nth("hh", b, j + 1))
                    v.tensor_tensor(hl[:, :, :], T_PS[:, 0:BW].rearrange("p (t n) -> p t n", t=TC), hh[:, :, :].bitcast(f32),
                                    ALU.subtract).then_inc(S["hl"], 1)
                return f

            def y_(b):
                dve.wait_ge(S["dn"], nth("dn", b, NJ))
                dve.wait_ge(S["x2r"], nth("x2r", b))
                if not is_first(b):
                    dve.wait_ge(S["out"], 16 * b)
                v.tensor_tensor(y[:, :], Y_PS[:, 0:D], x2r[:, :], ALU.add).then_inc(S["y"], 1)

            schedule(dve, {"split": split, "r1": r1, "r2": r2, "r4": r4, "r5": r5, "r6": r6, "r7": r7, "r9": r9, "r10": r10,
                           "r13": r13, "r14": r14, "r16": r16, "r18": r18, "r19": r19,
                           **{f"mx{u}": mx(u) for u in range(8)}, "c": c, "vt0": on(0), "vt1": on(1), "wo": wo_, "n3": n3, "xT": xT,
                           "gate1": gate1, "gate2": gate2, "gate3": gate3, "gate4": gate4, "y": y_,
                           **{f"ab{j}": ab(j) for j in range(NJ)}, **{f"T{j}": T_(j) for j in range(NJ)}})

        @block.tensor
        def _(pe):
            t = nc.tensor
            pe.wait_ge(S["w_small"], 12 * 16)
            for k in range(KC):
                last = t.matmul(R_PS[:, k * DC:(k + 1) * DC], l_tokv[:, k * P:(k + 1) * P], l_comp, start=True, stop=True)
            last.then_inc(S["setup_p"], 1)
            pe.wait_ge(S["setup_v"], 1)
            t.matmul(R_PS[0:DC, 128:128 + D], l_c2l, l_outres, start=True, stop=True).then_inc(S["setup_p"], 1)

            def halves(o, src):
                for k in range(KC):
                    last = t.transpose(o[:, k * P:(k + 1) * P], src[:, k * P:(k + 1) * P], ident)
                return last

            def product(o, xT, w):
                for k in range(KC):
                    last = t.matmul(o, xT[:, k * P:(k + 1) * P], w[:, k, :], start=k == 0, stop=k == KC - 1)
                return last

            def r3(b):
                if is_first(b):
                    pe.wait_ge(S["setup_a"], 2)
                else:
                    pe.wait_ge(S["KA"], nth("KA", b - 1))
                    pe.wait_ge(S["kloT"], nth("kloT", b - 1))
                pe.wait_ge(S["xn"], nth("xn", b))
                halves(R_PS, xn).then_inc(S["xnT"], 1)

            def r4(b):
                pe.wait_ge(S["xnT_sb"], nth("xnT_sb", b))
                product(R_PS[:, 0:DC], xnT, wc).then_inc(S["c"], 1)

            def r6(b):
                pe.wait_ge(S["chat"], nth("chat", b))
                t.transpose(R_PS[0:DC, 0:P], chat[:, :], ident).then_inc(S["chatT"], 1)

            def r7(b):
                pe.wait_ge(S["chT"], nth("chT", b))
                t.matmul(R_PS[:, 0:5 * DC], chT[:, :], wqkv_sb[:, :], start=True, stop=True).then_inc(S["qkv"], 1)

            def r8(b):
                pe.wait_ge(S["qk"], nth("qk", b))
                pe.wait_ge(S["v_sb"], nth("v_sb", b))
                for a in range(2):
                    last = t.transpose(R_PS[0:DC, a * P:(a + 1) * P], qk[:, a * DC:(a + 1) * DC], ident)
                last.then_inc(S["qkT"], 1)

            def r9(b):
                pe.wait_ge(S["qkT_sb"], nth("qkT_sb", b))
                if is_first(b):
                    pe.wait_ge(S["setup_g"], 12)
                t.matmul(R_PS[:, 0:P], qkT[:, 0, :], qkT[:, 1, :], start=True, stop=False)
                t.matmul(R_PS[:, 0:P], ident16[:, :], causal16[:, :], start=False, stop=True).then_inc(S["ss"], 1)

            def r11(b):
                pe.wait_ge(S["p"], nth("p", b))
                t.transpose(R_PS[:, 0:P], prob[:, :], ident).then_inc(S["pT"], 1)

            def r12(b):
                pe.wait_ge(S["pT_sb"], nth("pT_sb", b))
                t.matmul(R_PS[0:DC, 0:P], v_sb[:, :], probT[:, :], start=True, stop=True).then_inc(S["oT"], 1)

            def r13(b):
                pe.wait_ge(S["oT_sb"], nth("oT_sb", b))
                t.matmul(R_PS[:, 0:D], oT_sb[:, :], wback[:, :], start=True, stop=True).then_inc(S["o1"], 1)

            def r15(b):
                pe.wait_ge(S["x1n"], nth("x1n", b))
                halves(R_PS, x1n).then_inc(S["x1nT"], 1)

            def r16(b):
                pe.wait_ge(S["x1nT_sb"], nth("x1nT_sb", b))
                product(R_PS[:, 0:D], x1nT, wq_sb).then_inc(S["q"], 1)

            def r17(b):
                pe.wait_ge(S["qh"], nth("qh", b))
                pe.wait_ge(S["ql"], nth("ql", b))
                for h in range(HG):
                    last = t.transpose(R_PS[:, h * P:(h + 1) * P], qN[:, h, :, :].rearrange("p a c -> p (a c)").bitcast(f32), ident)
                last.then_inc(S["qT"], 1)

            def r18(b):
                pe.wait_ge(S["Q2"], nth("Q2", b))
                pe.wait_ge(S["ctx_in"], 16 * b + 16)
                for k in range(KC):
                    last = t.matmul(R_PS[:, 0:2 * GD], ctx_sb[:, k, :], wkv_sb[:, k, :], start=k == 0, stop=k == KC - 1)
                last.then_inc(S["kv"], 1)

            def r19(b):
                pe.wait_ge(S["kh"], nth("kh", b))
                pe.wait_ge(S["klo"], nth("klo", b))
                pe.wait_ge(S["va"], nth("va", b))
                t.transpose(R_PS[:, 0:P], kN[:, 0:2, :].rearrange("p a c -> p (a c)").bitcast(f32), ident)
                t.transpose(R_PS[0:GD, P:2 * P], kN[:, 2, :].bitcast(f32), ident).then_inc(S["kT"], 1)

            def ring(use, b):
                n = USES.index(use)
                if n >= 2:
                    name, k = READ[USES[n - 2]]
                    pe.wait_ge(S[name], nth(name, b, k))
                elif not is_first(b):
                    name, k = READ[USES[max(m for m in range(len(USES)) if m % 2 == n)]]
                    pe.wait_ge(S[name], nth(name, b - 1, k))
                return RING[n % 2]

            def mx(u):
                hg, hf = u % HG, u // HG
                def f(b):
                    o = ring(f"mx{u}", b)
                    if u == 0:
                        pe.wait_ge(S["KA"], nth("KA", b))
                        pe.wait_ge(S["Q2"], nth("Q2", b))
                        pe.wait_ge(S["pr2"], nth("pr2", b))
                    t.matmul(o[:, :], Q2[:, hg, :], KA[:, HG * hf:HG * hf + HG, :].rearrange("p g m -> p (g m)"), start=True, stop=False)
                    t.matmul(o[:, :], ident16[:, :], maskn[:, :].unsqueeze(1).to_broadcast([P, HG, P]), start=False, stop=True).then_inc(S["mx"], 1)
                return f

            def c(b):
                o = ring("c", b)
                pe.wait_ge(S["rmax"], nth("rmax", b, 8))
                t.transpose(o[:, 0:P], negc[:, :], ident).then_inc(S["cT"], 1)

            def s_(g):
                def f(b):
                    o = ring(f"s{g}", b)
                    if g == 0:
                        pe.wait_ge(S["Q3c"], nth("Q3c", b))
                        pe.wait_ge(S["Q3t"], nth("Q3t", b))
                        pe.wait_ge(S["KB"], nth("KB", b))
                        if is_first(b):
                            pe.wait_ge(S["setup_a"], 4)
                    t.matmul(o[:, :], KA[:, g, :], Q2[:, :, :].rearrange("p h n -> p (h n)"), start=True, stop=False)
                    t.matmul(o[:, :], KB[:, g, :], Q3[:, :, :].rearrange("p h n -> p (h n)"), start=False, stop=True).then_inc(S["s"], 1)
                return f

            def pv(n):
                def f(b):
                    if n > 0:
                        pe.wait_ge(S["vc"], nth("vc", b, n))
                    elif not is_first(b):
                        pe.wait_ge(S["vc"], nth("vc", b - 1, 2))
                    pe.wait_ge(S["pm"], nth("pm", b, NPT * n + NPT))
                    for k in range(NPT):
                        g = NPT * n + k
                        last = t.matmul(V_PS[32 * k:32 * k + 32, :], va[:, g * (HD + 1):g * (HD + 1) + 32],
                                        PT[:, slot(g), :, :].rearrange("p h n -> p (h n)"), start=True, stop=True)
                    last.then_inc(S["pv"], 1)
                return f

            def vt(n):
                def f(b):
                    o = ring(f"vt{n}", b)
                    pe.wait_ge(S["vc"], nth("vc", b, n + 1))
                    for h in range(HG):
                        last = t.transpose(o[:, h * P:(h + 1) * P], PT[:, n, h, :], ident)
                    last.then_inc(S["vt"], 1)
                return f

            def oT_(b):
                o = ring("oT", b)
                pe.wait_ge(S["on"], nth("on", b, 2))
                halves(o, o_nat).then_inc(S["oT2"], 1)

            def wo_(b):
                o = ring("wo", b)
                pe.wait_ge(S["oT2_sb"], nth("oT2_sb", b))
                product(o[:, 0:D], oT2, wo_sb).then_inc(S["wo"], 1)

            def xT(b):
                o = ring("xT", b)
                pe.wait_ge(S["x2n"], nth("x2n", b))
                halves(o, x2n).then_inc(S["xT"], 1)

            def three(o, hi, lo, whi, wlo, first, last_):
                t.matmul(o, hi, whi, start=first, stop=False)
                t.matmul(o, hi, wlo, start=False, stop=False)
                return t.matmul(o, lo, whi, start=False, stop=last_)

            def lg(b):
                o = ring("lg", b)
                if is_first(b):
                    pe.wait_ge(S["setup_v"], 2)
                pe.wait_ge(S["xl"], nth("xl", b))
                for k in range(KC):
                    last = three(o[:, 0:NE], xh[:, k, :], xl[:, k, :], gate_hi[:, k, :], gate_lo[:, k, :], k == 0, k == KC - 1)
                last.then_inc(S["lg"], 1)

            def gu(j):
                def f(b):
                    if is_first(b):
                        pe.wait_ge(S["w_lo"], 3 * j + 3)
                    if j > 0:
                        pe.wait_ge(S["av"], nth("av", b, j))
                    elif not is_first(b):
                        pe.wait_ge(S["av"], nth("av", b - 1, NJ))
                    for k in range(KC):
                        last = three(G_PS[:, 0:BW], xh[:, k, :], xl[:, k, :], wgu_hi[:, j, k, 0, :], wgu_lo[:, j, k, 0, :],
                                     k == 0, k == KC - 1)
                    last.then_inc(S["g"], 1)
                    if j > 0:
                        pe.wait_ge(S["bv"], nth("bv", b, j))
                    elif not is_first(b):
                        pe.wait_ge(S["bv"], nth("bv", b - 1, NJ))
                    for k in range(KC):
                        last = three(U_PS[:, 0:BW], xh[:, k, :], xl[:, k, :], wgu_hi[:, j, k, 1, :], wgu_lo[:, j, k, 1, :],
                                     k == 0, k == KC - 1)
                    last.then_inc(S["u"], 1)
                return f

            def T_(j):
                def f(b):
                    if j > 0:
                        pe.wait_ge(S["hl"], nth("hl", b, j))
                    elif not is_first(b):
                        pe.wait_ge(S["hl"], nth("hl", b - 1, NJ))
                    pe.wait_ge(S["h"], nth("h", b, j + 1))
                    for n in range(TC):
                        last = t.transpose(T_PS[:, n * P:(n + 1) * P], hv[:, n * P:(n + 1) * P], ident)
                    last.then_inc(S["T"], 1)
                return f

            def D_(j):
                def f(b):
                    if j == 0 and not is_first(b):
                        pe.wait_ge(S["y"], nth("y", b - 1))
                    pe.wait_ge(S["hl"], nth("hl", b, j + 1))
                    for n in range(TC):
                        last = three(Y_PS[:, 0:D], hh[:, n, :], hl[:, n, :], wd_hi[:, j, n, :], wd_lo[:, j, n, :],
                                     j == 0 and n == 0, j == NJ - 1 and n == TC - 1)
                    last.then_inc(S["dn"], 1)
                return f

            schedule(pe, {"r3": r3, "r4": r4, "r6": r6, "r7": r7, "r8": r8, "r9": r9, "r11": r11, "r12": r12, "r13": r13,
                          "r15": r15, "r16": r16, "r17": r17, "r18": r18, "r19": r19,
                          **{f"mx{u}": mx(u) for u in range(8)}, "c": c, **{f"s{g}": s_(g) for g in range(NG)},
                          **{f"pv{n}": pv(n) for n in range(2)}, **{f"vt{n}": vt(n) for n in range(2)}, "oT": oT_, "wo": wo_, "xT": xT, "lg": lg,
                          **{f"gu{j}": gu(j) for j in range(NJ)}, **{f"T{j}": T_(j) for j in range(NJ)},
                          **{f"D{j}": D_(j) for j in range(NJ)}})


def shape_constants(np):
    p = np.arange(P)
    c = np.zeros((P, CW), np.float32)
    c[:, 0:P] = np.eye(P)
    c[:, P:2 * P] = np.where(p[None, :] <= p[:, None], 0.0, -BIG)
    inv = (1.0 / np.float32(10000.0) ** (np.arange(0, DC, 2, dtype=np.float32) / np.float32(DC))).astype(np.float32)
    f = p.astype(np.float32)[:, None] * inv[None, :]
    cos, sin = np.concatenate([np.cos(f)] * 2, 1), np.concatenate([-np.sin(f), np.sin(f)], 1)
    scale = np.float32(1.0) / np.sqrt(np.float32(DC))
    at = 2 * P
    c[:, at:at + 2 * DC] = np.concatenate([cos * scale, cos], 1)
    c[:, at + 2 * DC:at + 4 * DC] = np.concatenate([sin * scale, sin], 1)
    at += 4 * DC
    c[:, at:at + NG] = (p[:, None] // HD) % NG == np.arange(NG)[None, :]
    c[:, at + NG:at + NG + HG] = p[:, None] % HG == np.arange(HG)[None, :]
    c[:, at + NG + HG:] = (p[:, None] % 32) // HG == np.arange(NG)[None, :]
    return c


def kernel(**inputs):
    import numpy as np
    import concourse.bacc as bacc
    from concourse import mybir as mb
    from concourse.bass_utils import run_bass_kernel_spmd as run

    a = {n: np.asarray(v) for n, v in inputs.items()}

    def cols(w):
        return w.T.reshape(KC, P, -1).transpose(1, 0, 2)

    wq, wkv = a["L0_attn_W_q_comp"].T, a["L0_attn_W_kv_comp"].T
    wk, wv = wkv[:, :DC], wkv[:, DC:]
    turn = np.concatenate([np.arange(DC // 2, DC), np.arange(DC // 2)])
    xq = a["L0_xattn_w_q"].reshape(NG, HG, HD, D).transpose(1, 0, 2, 3).reshape(D, D)
    arrays = {
        "x": a["x"],
        "ctxT": a["ctx_2048"].transpose(0, 2, 1).reshape(NB, KC, P, P).transpose(0, 2, 1, 3),
        "mask": a["mask_BxS2_if1"],
        "wgu": a["L0_ffn_gate_up_proj"].reshape(NJ, EJ, 2, NI, KC, P).transpose(5, 0, 4, 2, 1, 3).reshape(P, NJ, KC * 2 * BW),
        "wd": a["L0_ffn_down_proj"].transpose(0, 2, 1).reshape(NJ, TC, P, D).transpose(2, 0, 1, 3).reshape(P, NJ, TC * D),
        "gateT": cols(a["L0_ffn_gate_weight"]),
        "wtokv": a["L0_attn_W_to_kv"],
        "wcompT": a["L0_attn_W_compress"].T,
        "woutresT": a["L0_attn_W_out_res"].T,
        "wc2l": a["L0_attn_W_comp2lat"],
        "wqkv": np.concatenate([wq, wk, wq[:, turn], wk[:, turn], wv], 1),
        "gb": np.stack([a["L0_attn_ln_gamma"], a["L0_attn_ln_beta"]], 1),
        "bias2": np.broadcast_to(np.stack([a["L0_attn_b_out_res"], a["L0_xattn_b_o"]])[None], (P, 2, D)),
        "wq": cols(xq),
        "wkv": cols(np.concatenate([a["L0_xattn_w_k"], a["L0_xattn_w_v"]], 0)),
        "wo": cols(a["L0_xattn_w_o"]),
        "consts": shape_constants(np),
    }
    arrays = {n: np.ascontiguousarray(v) for n, v in arrays.items()}
    nc = bacc.Bacc("TRN2", target_bir_lowering=False, num_devices=1)
    args = {n: nc.dram_tensor(n + "_d", v.shape, mb.dt.from_np(v.dtype), kind="ExternalInput").ap() for n, v in arrays.items()}
    out = nc.dram_tensor("out_d", (NB, P, D), mb.dt.float32, kind="ExternalOutput").ap()
    decoder_kernel(nc, **args, out=out)
    r = run(nc, [{n + "_d": v for n, v in arrays.items()}], core_ids=[0])
    return r.results[0]["out_d"]
```

```python
import concourse.bass as bass
from concourse import mybir
from contextlib import ExitStack

NB, P, D = 16, 128, 256
KC = D // P
NE, NI = 32, 96
NJ, EJ = 8, 4
BW = EJ * NI
TC = BW // P
NG, HG, HD = 8, 4, 8
GD = NG * HD
DL, DC = 64, 32
CW = 2 * P + 4 * DC + NG + HG + NG
BIG = 1e30
EPS = 1e-5
NPT = 4
KEEP = 0.8


ORDER = """
0:gate8 0:gu0 0:res 0:gate9 0:gate10 0:gate11 0:gate12 0:h0 0:a0 0:gate13 0:b0 1:mx0 1:mx1 0:a1 0:h1 0:b1 0:gu1 0:T0
1:mx2 1:mx3 2:r2 0:h2 0:gu2 0:D0 0:a2 0:b2 0:T1 0:h3 1:mx4 0:a3 1:mx5 0:gu3 0:D1 0:b3 2:r3 1:mx6 1:mx7 0:T2 2:r4 0:gu4
1:c 0:D2 1:s0 2:r5 2:r6 0:a4 0:h4 0:b4 1:s1 0:T3 2:r7 1:s2 1:s3 0:gu5 2:r8 0:a5 0:D3 2:r9 2:r10 0:h5 0:T4 0:b5 1:s4
1:pv0 2:r11 1:s5 0:D4 1:vt0 2:r12 0:T5 1:s6 1:s7 2:r13 3:ldx 0:gu6 0:a6 0:b6 2:r14 1:pv1 0:D5 1:vt1 2:r15 0:h6 0:T6
1:oT 2:r16 1:wo 0:a7 0:b7 0:h7 0:gu7 2:r17 1:n3 0:D6 1:xT 2:r18 3:ldc 0:T7 1:lg 1:gate1 2:r19 3:r1 1:gate2 0:D7
1:gate3 1:gate4 1:gate5 1:gate6 1:gate7 0:y
""".split()
START = """
0:ldx 0:r1 0:r2 0:r3 0:r4 0:r5 0:r6 0:w 0:r7 1:w 2:w 0:r8 0:r9 3:w 0:ldc 0:r10 0:r11 4:w 0:r12 5:w 0:r13 1:ldx 0:gs
0:r14 0:r15 1:r1 6:w 7:w 0:r16 8:w 9:w 0:r17 1:r2 10:w 11:w 0:r18 0:r19 12:w 13:w 14:w 0:mx0 0:mx1 1:r3 15:w 0:mx2
16:w 0:mx3 17:w 18:w 0:mx4 19:w 1:r4 0:mx5 0:mx6 0:mx7 20:w 21:w 0:c 22:w 1:r5 23:w 1:ldc 0:s0 0:s1 1:r6 0:s2 1:r7
0:s3 1:r8 1:r9 1:r10 0:pv0 0:s4 0:s5 0:vt0 1:r11 0:s6 1:r12 0:s7 1:r13 2:ldx 0:pv1 1:r14 0:vt1 0:oT 2:r1 1:r15 0:wo
1:r16 1:r17 0:n3 0:xT 1:r18 2:ldc 2:r2 0:lg 0:gate1 0:gate2 0:gate3 1:r19 0:gate4 0:gate5 0:gate6 0:gate7 0:gate8
0:gate9 0:gate10 0:gate11 0:gate12 0:gu0 2:r3 0:a0 0:gate13 0:h0 0:b0 1:mx0 1:mx1 0:a1 2:r4 0:gu1 0:b1 0:T0 1:mx2 0:a2
0:h1 1:mx3 0:h2 0:b2 0:gu2 0:D0 1:mx4 0:T1 0:h3 2:r5 1:mx5 0:gu3 0:a3 1:mx6 0:D1 0:b3 1:mx7 0:T2 0:gu4 1:c 2:r6 0:D2
1:s0 2:r7 0:a4 0:b4 1:s1 0:T3 1:s2 0:a5 2:r8 1:s3 0:gu5 0:h4 2:r9 0:b5 2:r10 1:s4 1:pv0 1:s5 0:h5 0:D3 2:r11 1:vt0
0:T4 0:a6 2:r12 1:s6 0:b6 1:s7 0:gu6 0:res 2:r13 3:ldx 1:pv1 0:D4 0:h6 2:r14 0:T5 0:h7 1:vt1 3:r1 0:gu7 0:a7 1:oT 0:D5
0:b7 0:T6 2:r15 1:wo 2:r16 0:D6 2:r17 1:n3 1:xT 0:T7 2:r18 3:ldc 1:lg 1:gate1 2:r19 1:gate2 1:gate3 1:gate4 1:gate5
1:gate6 1:gate7 0:D7 0:y
""".split()
END = """
13:gu0 13:gate8 13:h0 13:gate9 13:gate10 13:a0 13:gate11 13:b0 13:gate12 13:gate13 14:mx0 13:h1 13:h2 13:a1 13:b1
14:mx1 13:gu1 13:T0 15:r2 13:a2 14:mx2 13:b2 13:gu2 13:D0 14:mx3 15:r3 13:T1 14:mx4 13:gu3 13:a3 14:mx5 15:r4 13:D1
13:b3 14:mx6 13:T2 14:mx7 13:a4 13:h3 15:r5 13:gu4 13:D2 13:b4 13:h4 13:T3 14:c 13:a5 13:gu5 15:r6 14:s0 14:s1 13:D3
13:b5 14:s2 15:r7 14:s3 13:gu6 15:r8 14:pv0 13:a6 14:s4 15:r9 15:r10 14:s5 13:h5 14:vt0 15:r11 13:T4 14:s6 15:r12
14:s7 15:r13 13:D4 13:res 15:r14 14:pv1 13:T5 15:r15 14:vt1 13:h6 15:r16 14:oT 13:D5 13:b6 14:wo 13:h7 14:n3 15:r17
13:T6 13:a7 13:gu7 14:xT 15:r18 14:lg 13:b7 14:gate1 14:gate2 15:r19 14:gate3 14:gate4 14:h0 14:gate5 14:gu0 14:gate6
14:h1 14:gate7 14:gate8 14:gate9 14:gate10 13:D6 14:gate11 14:gate12 14:a0 15:mx0 14:b0 13:T7 15:mx1 14:gate13 14:a1
14:gu1 15:mx2 13:D7 14:b1 15:mx3 13:y 14:T0 15:mx4 14:gu2 14:a2 14:h2 15:mx5 14:h3 14:b2 14:D0 14:T1 15:mx6 14:gu3
14:a3 15:mx7 14:D1 14:b3 14:res 14:T2 15:c 14:gu4 14:a4 15:s0 14:b4 15:s1 14:D2 15:s2 14:a5 15:s3 14:gu5 14:h4 14:T3
15:pv0 15:s4 15:s5 14:D3 15:vt0 14:b5 15:s6 14:T4 14:a6 15:s7 14:b6 14:gu6 15:pv1 14:h5 14:D4 15:vt1 15:oT 15:wo 14:T5
15:n3 14:a7 14:gu7 14:h6 15:xT 14:D5 14:b7 14:T6 15:lg 15:gate1 15:gate2 15:gate3 15:gate4 15:gu0 15:a0 15:gate5
15:gate6 15:gate7 15:b0 14:h7 15:h0 15:gate8 15:gate9 15:gate10 15:gate11 15:h1 15:h2 15:h3 14:D6 14:T7 15:gate12
15:gate13 15:gu1 15:a1 14:D7 15:b1 15:h4 15:T0 14:y 15:a2 15:b2 15:gu2 15:D0 15:T1 15:a3 15:b3 15:gu3 15:D1 15:T2
15:a4 15:gu4 15:D2 15:b4 15:T3 15:res 15:a5 15:b5 15:gu5 15:D3 15:T4 15:gu6 15:h5 15:D4 15:a6 15:b6 15:T5 15:a7 15:gu7
15:h6 15:b7 15:D5 15:T6 15:D6 15:T7 15:D7 15:y 15:h7
""".split()
ORDER, START, END = ([(s.split(":")[1], int(s.split(":")[0])) for s in order] for order in (ORDER, START, END))
AHEAD = max(n for _, n in ORDER)

READ = {**{f"mx{u}": ("rmax", u + 1) for u in range(8)}, "c": ("Q3c", 1), **{f"s{g}": ("e", g + 1) for g in range(NG)},
        **{f"vt{n}": ("on", n + 1) for n in range(2)}, "oT": ("oT2_sb", 1), "wo": ("x2", 1), "xT": ("xl", 1), "lg": ("eall", 1)}
USES = [(step, n) for step, n in ORDER if step in READ]
TURN = {step: k for k, (step, _) in enumerate(USES)}


def decoder_kernel(nc, x, ctxT, mask, wgu, wd, gateT, wtokv, wcompT, woutresT, wc2l, wqkv, gb, bias2,
                   wq, wkv, wo, consts, out):
    f32, f32r, bf16, i32 = mybir.dt.float32, mybir.dt.float32r, mybir.dt.bfloat16, mybir.dt.int32
    ALU, ACT, AX = mybir.AluOpType, mybir.ActivationFunctionType, mybir.AxisListType.X

    with ExitStack() as ctx:
        def sb(name, shape, dt=f32):
            return ctx.enter_context(nc.sbuf_tensor(name, shape, dt))

        scalars, used = sb("scalars", [P, 32]), iter(range(32))

        def one():
            n = next(used)
            return scalars[:, n:n + 1]

        wgu_hi, wgu_lo = (sb(n, [P, NJ, KC, 2, BW], f32r) for n in ("wgu_hi", "wgu_lo"))
        wd_hi, wd_lo = (sb(n, [P, NJ, TC, D], f32r) for n in ("wd_hi", "wd_lo"))
        gate_f = sb("gate_f", [P, KC, NE])
        gate_hi, gate_lo = (sb(n, [P, KC, NE], f32r) for n in ("gate_hi", "gate_lo"))
        con = sb("con", [P, CW])
        ident = con[:, 0:P]
        causal = con[:, P:2 * P]
        at0 = 2 * P
        cos = con[:, at0:at0 + 2 * DC]
        sin = con[:, at0 + 2 * DC:at0 + 4 * DC]
        at0 += 4 * DC
        own8 = con[:, at0:at0 + NG]
        own4 = con[:, at0 + NG:at0 + NG + HG]
        sel8 = con[:, at0 + NG + HG:at0 + 2 * NG + HG]
        ident16, causal16 = sb("ident16", [P, P], bf16), sb("causal16", [P, P], bf16)
        half, eps, zero, idle = (one() for _ in range(4))
        idle8 = sb("idle8", [P, 8])
        wc = sb("wc", [P, KC, DC])
        wback = sb("wback", [DC, D])
        wqkv_sb = sb("wqkv_sb", [DC, 5 * DC])
        gb_sb = sb("gb_sb", [DC, 2])
        bias_sb = sb("bias_sb", [P, 2, D])
        wq_sb, wo_sb = sb("wq_sb", [P, KC, D]), sb("wo_sb", [P, KC, D])
        wkv_sb = sb("wkv_sb", [P, KC, 2 * GD])
        xin, x1, x1b, xn, xnT = (sb(n, [P, D]) for n in ("xin", "x1", "x1b", "xn", "xnT"))
        x1n, x1nT = xn, xnT
        ctx_sb = sb("ctx_sb", [P, KC, P])
        mrow, mcol = sb("mrow", [P, P], i32), sb("mcol", [P, 1], i32)
        st = {n: sb("st_" + n, [P, 6]) for n in ("ln1", "lnc", "ln2", "ln3")}
        mv = {n: sb("mv_" + n, [P, 2]) for n in ("ln1", "lnc", "ln2", "ln3")}
        veps = {n: one() for n in ("ln1", "lnc", "ln2", "ln3")}
        rstd = {n: one() for n in ("ln1", "lnc", "ln2", "ln3")}
        chat, chT = sb("chat", [P, DC]), sb("chT", [DC, P])
        rope_s, qk = (sb(n, [P, 2 * DC]) for n in ("rope_s", "qk"))
        v_sb, qkT = sb("v_sb", [P, DC]), sb("qkT", [DC, 2, P])
        nmax, den, rden = (one() for _ in range(3))
        prob, probT, oT_sb = sb("prob", [P, P]), sb("probT", [P, P]), sb("oT_sb", [DC, P])
        qN = sb("qN", [P, HG, 2, GD], f32r)
        Q2 = sb("Q2", [P, HG, P], f32r)
        Q3 = sb("Q3", [96, HG, P], f32r)
        kN = sb("kN", [P, 3, GD], f32r)
        kloT = prob[0:GD, :]
        KA = sb("KA", [P, NG, P], f32r)
        KB = sb("KB", [96, NG, P], f32r)
        va = sb("va", [P, NG * (HD + 1) + 32])
        va_g = va[:, 0:NG * (HD + 1)].rearrange("p (g d) -> p g d", g=NG)
        padrow = mrow[:, :].bitcast(f32)
        maskn = sb("maskn", [P, P], bf16)
        padcol = one()
        negc = sb("negc", [P, P])
        PT = sb("PT", [P, NPT, HG, P])
        rdx = sb("rdx", [P, NG * HG])
        o_nat, oT2, x2, x2r = (sb(n, [P, D]) for n in ("o_nat", "oT2", "x2", "x2r"))
        x2n = o_nat
        xh, xl = sb("xh", [P, KC, P], f32r), sb("xl", [P, KC, P], f32r)
        nlmax, eall, e8 = one(), sb("eall", [P, NE]), sb("e8", [P, 8])
        tot, rtot, ksum, rk, thr = (one() for _ in range(5))
        cum = [sb(f"cum{n}", [P, 16]) for n in range(4)]
        kept, out8 = sb("kept", [P, 8]), sb("out8", [P, 8])
        ehalf, cm, ce = (sb(n, [P, NE]) for n in ("ehalf", "cm", "ce"))
        work = sb("work", [P, 4, BW])
        th, av, bv, hv = (work[:, n, :] for n in range(4))
        stage = [work[:, 2 * n:2 * n + 2, :].rearrange("p a n -> p (a n)") for n in range(2)]
        stage += [PT[:, :, :, :].rearrange("p s h n -> p (s h n)")[:, n * 2 * BW:(n + 1) * 2 * BW] for n in range(2)]
        hh, hl = sb("hh", [P, TC, P], f32r), sb("hl", [P, TC, P], f32r)
        y = sb("y", [P, D])
        l_tokv, l_outres = y[0:DL, :], x2r[0:DL, :]
        l_comp, l_c2l = oT2[0:DL, 0:DC], oT2[0:DL, DC:2 * DC]
        bank = [ctx.enter_context(nc.psum_tensor(f"bank{n}", [P, 512], f32)) for n in range(8)]
        G_PS, U_PS, T_PS, Y_PS, R_PS, V_PS = bank[0:6]
        RING = bank[6:8]

        def ring_bank(use):
            return RING[TURN[use] % 2]

        def slot(g):
            return g if g < NPT else (g + 1) % NPT

        PER = dict(mx=8, rmax=8, s=8, e=8, pm=8, pv=2, vc=2, vt=2, rdx=2, on=2, g=8, u=8, th=8, av=8, bv=8, h=8, T=8, hh=8, hl=8, dn=8)
        names = ("x_in ctx_in m_in w_first w_small w_bias w_more w_hi w_lo wd_lo gate_hi gate_lo setup_v setup_g setup_p wc wback sel "
                 "st1 mv1 ve1 rs1 xb xn xnT xnT_sb c stc mvc vec rsc chat chatT chT qkv rc rsn qk v_sb qkT qkT_sb "
                 "ss smax p rden pT pT_sb oT oT_sb o1 x1 st2 mv2 ve2 rs2 x1b x1n x1nT x1nT_sb q qh ql qT Q2 Q3t "
                 "kv kh klo va kT kloT KA KB pr pr2 pc "
                 "mx rmax cT Q3c s e pm pv vc vt rdx on oT2 oT2_sb wo x2 st3 mv3 ve3 rs3 x2n "
                 "x2r xT xh xl lg nlmax eall eh e8 tot rtot cu0 cu1 cu2 cu3 ksum out8a out8b thr rk cm ce "
                 "g u th av bv h T hh hl dn y out").split()
        S = {n: ctx.enter_context(nc.semaphore("s_" + n)) for n in names}
        S["w_in"] = [ctx.enter_context(nc.semaphore(f"s_w_in{j}")) for j in range(4)]

        def nth(name, b, k=1):
            return b * PER.get(name, 1) + k

        block = ctx.enter_context(nc.Block())

        def piece_of(gu, dn, piece):
            j, n = piece // 3, piece % 3
            return gu[:, j, n, :, :].rearrange("p g n -> p (g n)") if n < KC else dn[:, j, :, :].rearrange("p t n -> p (t n)")

        def split_done(eng, piece):
            if piece % 3 < KC:
                eng.wait_ge(S["w_lo"], KC * (piece // 3) + piece % 3 + 1)
            else:
                eng.wait_ge(S["wd_lo"], piece // 3 + 1)

        def is_first(b):
            return isinstance(b, int) and b == 0

        def schedule(eng, steps):
            def run(order, i=0):
                for step, n in order:
                    if step in steps:
                        steps[step](i + n)

            run(START)
            with eng.Fori(1, NB - AHEAD) as i:
                run(ORDER, i)
            run(END)

        def row(t, b):
            if isinstance(b, int):
                return t[b]
            return t[bass.ds(b, 1)].squeeze(0)

        @block.sync
        def _(sp):
            def small(name, *loads):
                for dst, src in loads:
                    sp.dma_start(dst, src).then_inc(S[name], 16)

            def ldx(b):
                if not is_first(b):
                    sp.wait_ge(S["x1"], nth("x1", b - 1))
                sp.dma_start(xin[:, :], row(x, b)).then_inc(S["x_in"], 16)
                if is_first(b):
                    small("w_first", (l_tokv, wtokv), (l_comp, wcompT), (con[:, :], consts))
                    small("w_small", (l_outres, woutresT), (l_c2l, wc2l), (wqkv_sb[:, :], wqkv), (gb_sb[:, :], gb))
                    small("w_bias", (bias_sb[:, :, :], bias2))

            def ldc(b):
                if not is_first(b):
                    sp.wait_ge(S["kv"], nth("kv", b - 1))
                    sp.wait_ge(S["pr2"], nth("pr2", b - 1))
                    sp.wait_ge(S["pc"], nth("pc", b - 1))
                sp.dma_start(ctx_sb[:, :, :], row(ctxT, b)).then_inc(S["ctx_in"], 16)
                sp.dma_start(mrow[:, :], row(mask, b).partition_broadcast(P)).then_inc(S["m_in"], 16)
                sp.dma_start(mcol[:, :], row(mask, b).rearrange("(p o) -> p o", o=1)).then_inc(S["m_in"], 16)

            def w(piece):
                if piece >= 4:
                    split_done(sp, piece - 4)
                j, n = piece // 3, piece % 3
                src = wgu[:, j, n * 2 * BW:(n + 1) * 2 * BW] if n < KC else wd[:, j, :]
                sp.dma_start(stage[piece % 4], src).then_inc(S["w_in"][piece % 4], 16)
                if piece == 3:
                    small("w_more", (wq_sb[:, :, :], wq), (wkv_sb[:, :, :], wkv), (wo_sb[:, :, :], wo), (gate_f[:, :, :], gateT))

            def store(b):
                sp.wait_ge(S["y"], nth("y", b))
                sp.dma_start(row(out, b), y[:, :]).then_inc(S["out"], 16)

            schedule(sp, {"w": w, "ldx": ldx, "ldc": ldc, "y": store})
            sp.wait_ge(S["out"], 16 * NB)

        @block.gpsimd
        def _(pool):
            gp = nc.gpsimd

            def landed():
                gp.tensor_tensor(idle[:, :], zero[:, :], zero[:, :], ALU.add)
            gp.memset(half[:, :], -0.5).then_inc(S["setup_g"], 1)
            gp.memset(eps[:, :], EPS).then_inc(S["setup_g"], 1)
            gp.memset(zero[:, :], 0.0).then_inc(S["setup_g"], 1)
            gp.memset(negc[:, :], 0.0).then_inc(S["setup_g"], 1)
            gp.memset(va[:, NG * (HD + 1):], 0.0).then_inc(S["setup_g"], 1)
            gp.memset(va_g[:, :, HD:HD + 1], 1.0).then_inc(S["setup_g"], 1)
            for c in cum:
                gp.memset(c[:, 0:8], 0.0).then_inc(S["setup_g"], 1)
            pool.wait_ge(S["setup_g"], 3)

            def inv_std(ln, sm, sv, sr, b):
                pool.wait_ge(S[sm], nth(sm, b))
                gp.tensor_tensor(veps[ln][:, :], mv[ln][:, 1:2], eps[:, :], ALU.add).then_inc(S[sv], 1)
                pool.wait_ge(S[sv], nth(sv, b))
                gp.tensor_tensor(rstd[ln][:, :], veps[ln][:, :], half[:, :], ALU.pow).then_inc(S[sr], 1)

            def w(piece):
                if piece % 3 == KC:
                    pool.wait_ge(S["w_hi"], piece + 1)
                    gp.tensor_tensor(piece_of(wgu_lo, wd_lo, piece), stage[piece % 4], piece_of(wgu_hi, wd_hi, piece).bitcast(f32), ALU.subtract).then_inc(S["wd_lo"], 1)

            def r1(b):
                inv_std("ln1", "mv1", "ve1", "rs1", b)

            def r2(b):
                if is_first(b):
                    pool.wait_ge(S["w_bias"], 16)
                pool.wait_ge(S["xn"], nth("xn", b))
                gp.tensor_tensor(xin[:, :], xin[:, :], bias_sb[:, 0, :], ALU.add).then_inc(S["xb"], 1)
                if is_first(b):
                    pool.wait_ge(S["w_first"], 3 * 16)
                    gp.tensor_copy(ident16[:, :], ident).then_inc(S["setup_g"], 1)
                    gp.tensor_copy(causal16[:, :], causal).then_inc(S["setup_g"], 1)

            def r4(b):
                inv_std("lnc", "mvc", "vec", "rsc", b)

            def r13(b):
                inv_std("ln2", "mv2", "ve2", "rs2", b)

            def r17(b):
                pool.wait_ge(S["x1"], nth("x1", b))
                if not is_first(b):
                    pool.wait_ge(S["x2"], nth("x2", b - 1))
                gp.tensor_tensor(x1b[:, :], x1[:, :], bias_sb[:, 1, :], ALU.add).then_inc(S["x1b"], 1)
                pool.wait_ge(S["Q2"], nth("Q2", b))
                gp.tensor_tensor(Q3[0:GD, :, :], Q2[0:GD, :, :].bitcast(f32), zero[0:GD, :].unsqueeze(2).to_broadcast([GD, HG, P]),
                                 ALU.add).then_inc(S["Q3t"], 1)

            def r18(b):
                if not is_first(b):
                    pool.wait_ge(S["rmax"], nth("rmax", b - 1, 8))
                pool.wait_ge(S["pr"], nth("pr", b))
                gp.tensor_tensor(maskn[:, :], padrow, causal, ALU.add).then_inc(S["pr2"], 1)

            def r19(b):
                pool.wait_ge(S["kloT"], nth("kloT", b))
                if not is_first(b):
                    pool.wait_ge(S["s"], nth("s", b - 1, 8))
                gp.tensor_tensor(KB[0:GD, :, :], kloT.unsqueeze(1).to_broadcast([GD, NG, P]),
                                 own8[0:GD, :].unsqueeze(2).to_broadcast([GD, NG, P]), ALU.mult).then_inc(S["KB"], 1)

            def s_(g):
                def f(b):
                    if g > 0:
                        pool.wait_ge(S["pm"], nth("pm", b, g))
                    elif not is_first(b):
                        pool.wait_ge(S["pm"], nth("pm", b - 1, NG))
                    pool.wait_ge(S["e"], nth("e", b, g + 1))
                    landed()
                    gp.affine_select(out=PT[:, slot(g), :, :], in_=PT[:, slot(g), :, :], compare_op=ALU.is_ge, fill=0.0, base=0,
                                     pattern=[[0, HG], [1, P]], channel_multiplier=-1).then_inc(S["pm"], 1)
                return f

            def wo_(b):
                inv_std("ln3", "mv3", "ve3", "rs3", b)

            def res(b):
                pool.wait_ge(S["x2"], nth("x2", b))
                if not is_first(b):
                    pool.wait_ge(S["y"], nth("y", b - 1))
                gp.tensor_tensor(x2r[:, :], x2[:, :], zero[:, :].to_broadcast([P, D]), ALU.add).then_inc(S["x2r"], 1)

            def h(j):
                def f(b):
                    pool.wait_ge(S["bv"], nth("bv", b, j + 1))
                    pool.wait_ge(S["ce"], nth("ce", b))
                    if j > 0:
                        pool.wait_ge(S["T"], nth("T", b, j))
                    elif not is_first(b):
                        pool.wait_ge(S["T"], nth("T", b - 1, NJ))
                    gp.tensor_tensor(hv.rearrange("p (e i) -> p e i", e=EJ), bv.rearrange("p (e i) -> p e i", e=EJ),
                                     ce[:, EJ * j:EJ * j + EJ].unsqueeze(2).to_broadcast([P, EJ, NI]), ALU.mult).then_inc(S["h"], 1)
                return f

            schedule(pool, {"w": w, "r1": r1, "r2": r2, "r4": r4, "r13": r13, "r17": r17, "r18": r18, "r19": r19, "wo": wo_, "res": res,
                            **{f"s{g}": s_(g) for g in range(NG)}, **{f"h{j}": h(j) for j in range(NJ)}})

        @block.scalar
        def _(act):
            ac = nc.scalar

            def copy(o, i):
                return ac.activation(o, i, ACT.Copy)

            act.wait_ge(S["setup_p"], 1)
            copy(wc[:, :, :], Y_PS[:, 0:KC * DC].rearrange("p (k c) -> p k c", k=KC)).then_inc(S["wc"], 1)

            def w(piece):
                act.wait_ge(S["w_in"][piece % 4], 16 * (piece // 4 + 1))
                copy(piece_of(wgu_hi, wd_hi, piece), stage[piece % 4]).then_inc(S["w_hi"], 1)

            def gs(_):
                act.wait_ge(S["w_more"], 4 * 16)
                copy(gate_hi[:, :, :], gate_f[:, :, :]).then_inc(S["gate_hi"], 1)
                copy(KB[GD:96, :, :], sel8[GD:96, :].unsqueeze(2).to_broadcast([32, NG, P])).then_inc(S["sel"], 1)

            def r3(b):
                act.wait_ge(S["xnT"], nth("xnT", b))
                copy(xnT[:, :], R_PS[:, 0:D]).then_inc(S["xnT_sb"], 1)

            def r8(b):
                act.wait_ge(S["qkT"], nth("qkT", b))
                copy(qkT[:, :, :], R_PS[0:DC, 0:2 * P].rearrange("p (a n) -> p a n", a=2)).then_inc(S["qkT_sb"], 1)
                if is_first(b):
                    act.wait_ge(S["setup_p"], 2)
                    copy(wback[:, :], V_PS[0:DC, 0:D]).then_inc(S["wback"], 1)

            def r10(b):
                act.wait_ge(S["smax"], nth("smax", b))
                ac.activation(prob[:, :], R_PS[:, 0:P], ACT.Exp, bias=nmax[:, :], accum_out=den[:, :]).then_inc(S["p"], 1)

            def r11(b):
                act.wait_ge(S["pT"], nth("pT", b))
                copy(probT[:, :], R_PS[:, 0:P]).then_inc(S["pT_sb"], 1)

            def r12(b):
                act.wait_ge(S["oT"], nth("oT", b))
                copy(oT_sb[:, :], R_PS[0:DC, 0:P]).then_inc(S["oT_sb"], 1)

            def r15(b):
                act.wait_ge(S["x1nT"], nth("x1nT", b))
                copy(x1nT[:, :], R_PS[:, 0:D]).then_inc(S["x1nT_sb"], 1)

            def r16(b):
                act.wait_ge(S["q"], nth("q", b))
                copy(qN[:, :, 0, :], R_PS[:, 0:D].rearrange("p (h c) -> p h c", h=HG)).then_inc(S["qh"], 1)

            def r17(b):
                act.wait_ge(S["qT"], nth("qT", b))
                if not is_first(b):
                    act.wait_ge(S["s"], nth("s", b - 1, 8))
                copy(Q2[:, :, :], R_PS[:, :].rearrange("p (h n) -> p h n", h=HG)).then_inc(S["Q2"], 1)

            def r18(b):
                act.wait_ge(S["kv"], nth("kv", b))
                copy(kN[:, 0:2, :], R_PS[:, 0:GD].unsqueeze(1).to_broadcast([P, 2, GD])).then_inc(S["kh"], 1)
                if is_first(b):
                    act.wait_ge(S["setup_g"], 6)
                else:
                    act.wait_ge(S["pv"], nth("pv", b - 1, 2))
                copy(va_g[:, :, 0:HD], R_PS[:, GD:2 * GD].rearrange("p (g d) -> p g d", g=NG)).then_inc(S["va"], 1)

            def r19(b):
                act.wait_ge(S["kT"], nth("kT", b))
                if not is_first(b):
                    act.wait_ge(S["KB"], nth("KB", b - 1))
                copy(kloT, R_PS[0:GD, P:2 * P]).then_inc(S["kloT"], 1)
                if not is_first(b):
                    act.wait_ge(S["s"], nth("s", b - 1, 8))
                for g in range(NG):
                    last = ac.activation(KA[:, g, :], R_PS[:, 0:P], ACT.Copy, scale=own8[:, g:g + 1])
                last.then_inc(S["KA"], 1)

            def s_(g):
                def f(b):
                    act.wait_ge(S["s"], nth("s", b, g + 1))
                    if g == 0:
                        act.wait_ge(S["pc"], nth("pc", b))
                        if is_first(b):
                            split_done(act, 3 * NJ - 2)
                            split_done(act, 3 * NJ - 1)
                    if g == NPT:
                        act.wait_ge(S["pv"], nth("pv", b))
                    if g == NG - 1:
                        act.wait_ge(S["vt"], nth("vt", b))
                    ac.activation(PT[:, slot(g), :, :].rearrange("p h n -> p (h n)"), ring_bank(f"s{g}")[:, :], ACT.Exp,
                                  bias=padcol[:, :], scale=float(HD) ** -0.5).then_inc(S["e"], 1)
                return f

            def pv(n):
                def f(b):
                    act.wait_ge(S["pv"], nth("pv", b, n + 1))
                    copy(PT[:, n, :, :].rearrange("p h n -> p (h n)"), V_PS[:, :]).then_inc(S["vc"], 1)
                return f

            def oT_(b):
                act.wait_ge(S["oT2"], nth("oT2", b))
                copy(oT2[:, :], ring_bank("oT")[:, 0:D]).then_inc(S["oT2_sb"], 1)

            def xT(b):
                act.wait_ge(S["xT"], nth("xT", b))
                if not is_first(b):
                    act.wait_ge(S["u"], nth("u", b - 1, NJ))
                copy(xh[:, :, :], ring_bank("xT")[:, 0:D].rearrange("p (k n) -> p k n", k=KC)).then_inc(S["xh"], 1)

            def gate1(b):
                act.wait_ge(S["nlmax"], nth("nlmax", b))
                ac.activation(eall[:, :], ring_bank("lg")[:, 0:NE], ACT.Exp, bias=nlmax[:, :]).then_inc(S["eall"], 1)

            def gu(j):
                def f(b):
                    if j == 0 and is_first(b):
                        split_done(act, 3 * NJ - 2)
                        split_done(act, 3 * NJ - 1)
                    act.wait_ge(S["g"], nth("g", b, j + 1))
                    ac.activation(th, G_PS[:, 0:BW], ACT.Tanh, scale=0.5).then_inc(S["th"], 1)
                return f

            def T_(j):
                def f(b):
                    act.wait_ge(S["T"], nth("T", b, j + 1))
                    if j > 0:
                        act.wait_ge(S["dn"], nth("dn", b, j))
                    elif not is_first(b):
                        act.wait_ge(S["dn"], nth("dn", b - 1, NJ))
                    copy(hh[:, :, :], T_PS[:, 0:BW].rearrange("p (t n) -> p t n", t=TC)).then_inc(S["hh"], 1)
                return f

            schedule(act, {"w": w, "gs": gs, "r3": r3, "r8": r8, "r10": r10, "r11": r11, "r12": r12, "r15": r15,
                           "r16": r16, "r17": r17, "r18": r18, "r19": r19, "oT": oT_, "xT": xT, "gate1": gate1, "pv0": pv(0), "pv1": pv(1),
                           **{f"s{g}": s_(g) for g in range(NG)},
                           **{f"gu{j}": gu(j) for j in range(NJ)}, **{f"T{j}": T_(j) for j in range(NJ)}})

        @block.vector
        def _(dve):
            v = nc.vector

            def stats(ln, src, ss, sm, b):
                v.bn_stats(st[ln][:, :], src).then_inc(S[ss], 1)
                dve.drain()
                v.bn_aggr(mv[ln][:, :], st[ln][:, :]).then_inc(S[sm], 1)

            def normal(ln, o, src):
                return v.tensor_scalar(o, src, mv[ln][:, 0:1], rstd[ln][:, :], ALU.subtract, ALU.mult)

            def w(piece):
                if piece % 3 < KC:
                    dve.wait_ge(S["w_hi"], piece + 1)
                    v.tensor_tensor(piece_of(wgu_lo, wd_lo, piece), stage[piece % 4], piece_of(wgu_hi, wd_hi, piece).bitcast(f32), ALU.subtract).then_inc(S["w_lo"], 1)

            def gs(_):
                dve.wait_ge(S["gate_hi"], 1)
                v.tensor_tensor(gate_lo[:, :, :], gate_f[:, :, :], gate_hi[:, :, :].bitcast(f32), ALU.subtract).then_inc(S["gate_lo"], 1)

            def r1(b):
                dve.wait_ge(S["x_in"], 16 * b + 16)
                stats("ln1", xin[:, :], "st1", "mv1", b)

            def r2(b):
                dve.wait_ge(S["rs1"], nth("rs1", b))
                normal("ln1", xn[:, :], xin[:, :]).then_inc(S["xn"], 1)
                if is_first(b):
                    dve.wait_ge(S["w_first"], 3 * 16)
                    dve.wait_ge(S["w_small"], 4 * 16)
                    v.tensor_tensor(l_outres, l_outres, l_tokv, ALU.add).then_inc(S["setup_v"], 1)

            def r4(b):
                dve.wait_ge(S["c"], nth("c", b))
                stats("lnc", R_PS[:, 0:DC], "stc", "mvc", b)

            def r5(b):
                dve.wait_ge(S["rsc"], nth("rsc", b))
                normal("lnc", chat[:, :], R_PS[:, 0:DC]).then_inc(S["chat"], 1)

            def r6(b):
                dve.wait_ge(S["chatT"], nth("chatT", b))
                v.tensor_scalar(chT[:, :], R_PS[0:DC, 0:P], gb_sb[:, 0:1], gb_sb[:, 1:2], ALU.mult, ALU.add).then_inc(S["chT"], 1)

            def r7(b):
                dve.wait_ge(S["qkv"], nth("qkv", b))
                v.tensor_tensor(qk[:, :], R_PS[:, 0:2 * DC], cos, ALU.mult).then_inc(S["rc"], 1)
                v.tensor_tensor(rope_s[:, :], R_PS[:, 2 * DC:4 * DC], sin, ALU.mult).then_inc(S["rsn"], 1)
                v.tensor_copy(v_sb[:, :], R_PS[:, 4 * DC:5 * DC]).then_inc(S["v_sb"], 1)
                dve.wait_ge(S["rc"], nth("rc", b))
                dve.wait_ge(S["rsn"], nth("rsn", b))
                v.tensor_tensor(qk[:, :], qk[:, :], rope_s[:, :], ALU.add).then_inc(S["qk"], 1)

            def r9(b):
                dve.wait_ge(S["ss"], nth("ss", b))
                v.tensor_reduce(nmax[:, :], R_PS[:, 0:P], AX, ALU.max, negate=True).then_inc(S["smax"], 1)

            def r10(b):
                dve.wait_ge(S["p"], nth("p", b))
                v.reciprocal(rden[:, :], den[:, :]).then_inc(S["rden"], 1)

            def r13(b):
                dve.wait_ge(S["o1"], nth("o1", b))
                dve.wait_ge(S["rden"], nth("rden", b))
                dve.wait_ge(S["xb"], nth("xb", b))
                if not is_first(b):
                    dve.wait_ge(S["x1b"], nth("x1b", b - 1))
                v.scalar_tensor_tensor(x1[:, :], R_PS[:, 0:D], rden[:, :], xin[:, :], ALU.mult, ALU.add).then_inc(S["x1"], 1)
                dve.wait_ge(S["x1"], nth("x1", b))
                stats("ln2", x1[:, :], "st2", "mv2", b)

            def r14(b):
                dve.wait_ge(S["rs2"], nth("rs2", b))
                normal("ln2", x1n[:, :], x1[:, :]).then_inc(S["x1n"], 1)

            def r16(b):
                dve.wait_ge(S["qh"], nth("qh", b))
                v.tensor_tensor(qN[:, :, 1, :], R_PS[:, 0:D].rearrange("p (h c) -> p h c", h=HG),
                                qN[:, :, 0, :].bitcast(f32), ALU.subtract).then_inc(S["ql"], 1)

            def r18(b):
                dve.wait_ge(S["m_in"], 32 * b + 32)
                v.tensor_scalar(padrow, mrow[:, :], 0.0, -BIG, ALU.is_equal, ALU.mult).then_inc(S["pr"], 1)
                if not is_first(b):
                    dve.wait_ge(S["e"], nth("e", b - 1, 8))
                v.tensor_scalar(padcol[:, :], mcol[:, :], 0.0, -BIG, ALU.is_equal, ALU.mult).then_inc(S["pc"], 1)
                dve.wait_ge(S["va"], nth("va", b))
                v.tensor_tensor(kN[:, 2, :], R_PS[:, 0:GD], kN[:, 0, :].bitcast(f32), ALU.subtract).then_inc(S["klo"], 1)

            def mx(u):
                hg, hf = u % HG, u // HG
                def f(b):
                    if u == 0 and is_first(b):
                        dve.wait_ge(S["setup_g"], 4)
                    if u == 0:
                        dve.wait_ge(S["pr2"], nth("pr2", b))
                    dve.wait_ge(S["mx"], nth("mx", b, u + 1))
                    v.tensor_tensor(idle8[:, u:u + 1], zero[:, :], zero[:, :], ALU.add)
                    for k in range(HG):
                        scores = ring_bank(f"mx{u}")[:, k * P:(k + 1) * P]
                        at = GD + HG * (HG * hf + k) + hg
                        last = v.tensor_tensor_reduce(scores, scores, maskn[:, :], -1.0, 3 * BIG, ALU.add, ALU.min, negc[:, at:at + 1])
                    last.then_inc(S["rmax"], 1)
                return f

            def c(b):
                dve.wait_ge(S["cT"], nth("cT", b))
                v.tensor_tensor(Q3[GD:96, :, :], ring_bank("c")[GD:96, 0:P].unsqueeze(1).to_broadcast([32, HG, P]),
                                own4[GD:96, :].unsqueeze(2).to_broadcast([32, HG, P]), ALU.mult).then_inc(S["Q3c"], 1)

            def on(n):
                def f(b):
                    heads = ring_bank(f"vt{n}")[:, :].rearrange("p (h g d) -> p g h d", h=HG, g=NPT)
                    rd = rdx[:, :].rearrange("p (n g h) -> p n g h", n=2, g=NPT)[:, n, :, :].unsqueeze(3)
                    dve.wait_ge(S["vt"], nth("vt", b, n + 1))
                    v.reciprocal(rd, heads[:, :, :, HD:HD + 1]).then_inc(S["rdx"], 1)
                    dve.wait_ge(S["rdx"], nth("rdx", b, n + 1))
                    v.tensor_tensor(o_nat[:, n * P:(n + 1) * P].rearrange("p (g h d) -> p g h d", g=NPT, h=HG), heads[:, :, :, 0:HD],
                                    rd.to_broadcast([P, NPT, HG, HD]), ALU.mult).then_inc(S["on"], 1)
                return f

            def wo_(b):
                dve.wait_ge(S["wo"], nth("wo", b))
                dve.wait_ge(S["x1b"], nth("x1b", b))
                if not is_first(b):
                    dve.wait_ge(S["x2r"], nth("x2r", b - 1))
                v.tensor_tensor(x2[:, :], ring_bank("wo")[:, 0:D], x1b[:, :], ALU.add).then_inc(S["x2"], 1)
                dve.wait_ge(S["x2"], nth("x2", b))
                stats("ln3", x2[:, :], "st3", "mv3", b)

            def n3(b):
                dve.wait_ge(S["rs3"], nth("rs3", b))
                normal("ln3", x2n[:, :], x2[:, :]).then_inc(S["x2n"], 1)

            def xT(b):
                dve.wait_ge(S["xh"], nth("xh", b))
                v.tensor_tensor(xl[:, :, :], ring_bank("xT")[:, 0:D].rearrange("p (k n) -> p k n", k=KC), xh[:, :, :].bitcast(f32),
                                ALU.subtract).then_inc(S["xl"], 1)

            def gate1(b):
                dve.wait_ge(S["lg"], nth("lg", b))
                v.tensor_reduce(nlmax[:, :], ring_bank("lg")[:, 0:NE], AX, ALU.max, negate=True).then_inc(S["nlmax"], 1)

            def gate2(b):
                if is_first(b):
                    dve.wait_ge(S["setup_g"], 10)
                dve.wait_ge(S["eall"], nth("eall", b))
                v.tensor_scalar(ehalf[:, :], eall[:, :], 0.5, None, ALU.mult).then_inc(S["eh"], 1)
                v.max(e8[:, :], eall[:, :]).then_inc(S["e8"], 1)

            def gate3(b):
                dve.wait_ge(S["e8"], nth("e8", b))
                v.reduce_sum(tot[:, :], e8[:, :], AX).then_inc(S["tot"], 1)

            def gate4(b):
                dve.wait_ge(S["tot"], nth("tot", b))
                v.reciprocal(rtot[:, :], tot[:, :]).then_inc(S["rtot"], 1)

            def gate5(b):
                dve.wait_ge(S["rtot"], nth("rtot", b))
                v.tensor_scalar(cum[0][:, 8:16], e8[:, :], rtot[:, :], None, ALU.mult).then_inc(S["cu0"], 1)

            def sums(n):
                def f(b):
                    by = 2 ** n
                    dve.wait_ge(S[f"cu{n}"], nth(f"cu{n}", b))
                    v.tensor_tensor(cum[n + 1][:, 8:16], cum[n][:, 8:16], cum[n][:, 8 - by:16 - by], ALU.add).then_inc(S[f"cu{n + 1}"], 1)
                return f

            def gate9(b):
                dve.wait_ge(S["cu3"], nth("cu3", b))
                v.scalar_tensor_tensor(kept[:, :], cum[3][:, 7:15], KEEP, e8[:, :], ALU.is_lt, ALU.mult,
                                       accum_out=ksum[:, :]).then_inc(S["ksum"], 1)
                v.tensor_scalar(out8[:, :], cum[3][:, 7:15], KEEP, 4.0, ALU.is_ge, ALU.mult).then_inc(S["out8a"], 1)

            def gate10(b):
                dve.wait_ge(S["out8a"], nth("out8a", b))
                v.tensor_tensor(out8[:, :], out8[:, :], e8[:, :], ALU.add).then_inc(S["out8b"], 1)
                dve.wait_ge(S["ksum"], nth("ksum", b))
                v.reciprocal(rk[:, :], ksum[:, :]).then_inc(S["rk"], 1)

            def gate11(b):
                dve.wait_ge(S["out8b"], nth("out8b", b))
                v.tensor_reduce(thr[:, :], out8[:, :], AX, ALU.min).then_inc(S["thr"], 1)

            def gate12(b):
                dve.wait_ge(S["thr"], nth("thr", b))
                dve.wait_ge(S["eh"], nth("eh", b))
                v.scalar_tensor_tensor(cm[:, :], eall[:, :], thr[:, :], ehalf[:, :], ALU.is_ge, ALU.mult).then_inc(S["cm"], 1)

            def gate13(b):
                dve.wait_ge(S["cm"], nth("cm", b))
                dve.wait_ge(S["rk"], nth("rk", b))
                if not is_first(b):
                    dve.wait_ge(S["h"], nth("h", b - 1, NJ))
                v.tensor_scalar(ce[:, :], cm[:, :], rk[:, :], None, ALU.mult).then_inc(S["ce"], 1)

            def a(j):
                def f(b):
                    dve.wait_ge(S["th"], nth("th", b, j + 1))
                    if j > 0:
                        dve.wait_ge(S["bv"], nth("bv", b, j))
                    elif not is_first(b):
                        dve.wait_ge(S["bv"], nth("bv", b - 1, NJ))
                    v.scalar_tensor_tensor(av, th, 1.0, G_PS[:, 0:BW], ALU.add, ALU.mult).then_inc(S["av"], 1)
                return f

            def b_(j):
                def f(b):
                    dve.wait_ge(S["av"], nth("av", b, j + 1))
                    dve.wait_ge(S["u"], nth("u", b, j + 1))
                    if j > 0:
                        dve.wait_ge(S["h"], nth("h", b, j))
                    elif not is_first(b):
                        dve.wait_ge(S["h"], nth("h", b - 1, NJ))
                    v.tensor_tensor(bv, av, U_PS[:, 0:BW], ALU.mult).then_inc(S["bv"], 1)
                return f

            def T_(j):
                def f(b):
                    dve.wait_ge(S["hh"], nth("hh", b, j + 1))
                    v.tensor_tensor(hl[:, :, :], T_PS[:, 0:BW].rearrange("p (t n) -> p t n", t=TC), hh[:, :, :].bitcast(f32),
                                    ALU.subtract).then_inc(S["hl"], 1)
                return f

            def y_(b):
                dve.wait_ge(S["dn"], nth("dn", b, NJ))
                dve.wait_ge(S["x2r"], nth("x2r", b))
                if not is_first(b):
                    dve.wait_ge(S["out"], 16 * b)
                v.tensor_tensor(y[:, :], Y_PS[:, 0:D], x2r[:, :], ALU.add).then_inc(S["y"], 1)

            schedule(dve, {"w": w, "gs": gs, "r1": r1, "r2": r2, "r4": r4, "r5": r5, "r6": r6, "r7": r7, "r9": r9, "r10": r10,
                           "r13": r13, "r14": r14, "r16": r16, "r18": r18,
                           **{f"mx{u}": mx(u) for u in range(8)}, "c": c, "vt0": on(0), "vt1": on(1), "wo": wo_, "n3": n3, "xT": xT,
                           "gate1": gate1, "gate2": gate2, "gate3": gate3, "gate4": gate4, "y": y_,
                           "gate5": gate5, **{f"gate{6 + n}": sums(n) for n in range(3)}, "gate9": gate9, "gate10": gate10,
                           "gate11": gate11, "gate12": gate12, "gate13": gate13,
                           **{f"a{j}": a(j) for j in range(NJ)}, **{f"b{j}": b_(j) for j in range(NJ)}, **{f"T{j}": T_(j) for j in range(NJ)}})

        @block.tensor
        def _(pe):
            t = nc.tensor
            pe.wait_ge(S["w_first"], 3 * 16)
            for k in range(KC):
                last = t.matmul(Y_PS[:, k * DC:(k + 1) * DC], l_tokv[:, k * P:(k + 1) * P], l_comp, start=True, stop=True)
            last.then_inc(S["setup_p"], 1)

            def halves(o, src):
                for k in range(KC):
                    last = t.transpose(o[:, k * P:(k + 1) * P], src[:, k * P:(k + 1) * P], ident)
                return last

            def product(o, xT, w):
                for k in range(KC):
                    last = t.matmul(o, xT[:, k * P:(k + 1) * P], w[:, k, :], start=k == 0, stop=k == KC - 1)
                return last

            def r3(b):
                if not is_first(b):
                    pe.wait_ge(S["KA"], nth("KA", b - 1))
                pe.wait_ge(S["xn"], nth("xn", b))
                halves(R_PS, xn).then_inc(S["xnT"], 1)

            def r4(b):
                if is_first(b):
                    pe.wait_ge(S["wc"], 1)
                pe.wait_ge(S["xnT_sb"], nth("xnT_sb", b))
                product(R_PS[:, 0:DC], xnT, wc).then_inc(S["c"], 1)
                if is_first(b):
                    pe.wait_ge(S["setup_v"], 1)
                    t.matmul(V_PS[0:DC, 0:D], l_c2l, l_outres, start=True, stop=True).then_inc(S["setup_p"], 1)

            def r6(b):
                pe.wait_ge(S["chat"], nth("chat", b))
                t.transpose(R_PS[0:DC, 0:P], chat[:, :], ident).then_inc(S["chatT"], 1)

            def r7(b):
                pe.wait_ge(S["chT"], nth("chT", b))
                t.matmul(R_PS[:, 0:5 * DC], chT[:, :], wqkv_sb[:, :], start=True, stop=True).then_inc(S["qkv"], 1)

            def r8(b):
                pe.wait_ge(S["qk"], nth("qk", b))
                pe.wait_ge(S["v_sb"], nth("v_sb", b))
                for a in range(2):
                    last = t.transpose(R_PS[0:DC, a * P:(a + 1) * P], qk[:, a * DC:(a + 1) * DC], ident)
                last.then_inc(S["qkT"], 1)

            def r9(b):
                pe.wait_ge(S["qkT_sb"], nth("qkT_sb", b))
                if is_first(b):
                    pe.wait_ge(S["setup_g"], 12)
                t.matmul(R_PS[:, 0:P], qkT[:, 0, :], qkT[:, 1, :], start=True, stop=False)
                t.matmul(R_PS[:, 0:P], ident16[:, :], causal16[:, :], start=False, stop=True).then_inc(S["ss"], 1)

            def r11(b):
                pe.wait_ge(S["p"], nth("p", b))
                t.transpose(R_PS[:, 0:P], prob[:, :], ident).then_inc(S["pT"], 1)

            def r12(b):
                pe.wait_ge(S["pT_sb"], nth("pT_sb", b))
                t.matmul(R_PS[0:DC, 0:P], v_sb[:, :], probT[:, :], start=True, stop=True).then_inc(S["oT"], 1)

            def r13(b):
                if is_first(b):
                    pe.wait_ge(S["wback"], 1)
                pe.wait_ge(S["oT_sb"], nth("oT_sb", b))
                t.matmul(R_PS[:, 0:D], oT_sb[:, :], wback[:, :], start=True, stop=True).then_inc(S["o1"], 1)

            def r15(b):
                pe.wait_ge(S["x1n"], nth("x1n", b))
                halves(R_PS, x1n).then_inc(S["x1nT"], 1)

            def r16(b):
                if is_first(b):
                    pe.wait_ge(S["w_more"], 4 * 16)
                pe.wait_ge(S["x1nT_sb"], nth("x1nT_sb", b))
                product(R_PS[:, 0:D], x1nT, wq_sb).then_inc(S["q"], 1)

            def r17(b):
                pe.wait_ge(S["qh"], nth("qh", b))
                pe.wait_ge(S["ql"], nth("ql", b))
                for h in range(HG):
                    last = t.transpose(R_PS[:, h * P:(h + 1) * P], qN[:, h, :, :].rearrange("p a c -> p (a c)").bitcast(f32), ident)
                last.then_inc(S["qT"], 1)

            def r18(b):
                pe.wait_ge(S["Q2"], nth("Q2", b))
                pe.wait_ge(S["ctx_in"], 16 * b + 16)
                for k in range(KC):
                    last = t.matmul(R_PS[:, 0:2 * GD], ctx_sb[:, k, :], wkv_sb[:, k, :], start=k == 0, stop=k == KC - 1)
                last.then_inc(S["kv"], 1)

            def r19(b):
                pe.wait_ge(S["kh"], nth("kh", b))
                pe.wait_ge(S["klo"], nth("klo", b))
                pe.wait_ge(S["va"], nth("va", b))
                t.transpose(R_PS[:, 0:P], kN[:, 0:2, :].rearrange("p a c -> p (a c)").bitcast(f32), ident)
                t.transpose(R_PS[0:GD, P:2 * P], kN[:, 2, :].bitcast(f32), ident).then_inc(S["kT"], 1)

            def ring(use, b):
                n, back = TURN[use], 0
                while True:
                    m = n - 2
                    if m < 0:
                        m, back = max(k for k in range(len(USES)) if k % 2 == n % 2), back + 1
                    n = m
                    of = b + (USES[n][1] - USES[TURN[use]][1] - back)
                    if not isinstance(of, int) or 0 <= of < NB:
                        break
                    if of < 0 and back > AHEAD:
                        return ring_bank(use)
                name, k = READ[USES[n][0]]
                pe.wait_ge(S[name], nth(name, of, k))
                return ring_bank(use)

            def mx(u):
                hg, hf = u % HG, u // HG
                def f(b):
                    o = ring(f"mx{u}", b)
                    if u == 0:
                        pe.wait_ge(S["KA"], nth("KA", b))
                        pe.wait_ge(S["Q2"], nth("Q2", b))
                    t.matmul(o[:, :], Q2[:, hg, :], KA[:, HG * hf:HG * hf + HG, :].rearrange("p g m -> p (g m)"), start=True, stop=True).then_inc(S["mx"], 1)
                return f

            def c(b):
                o = ring("c", b)
                pe.wait_ge(S["rmax"], nth("rmax", b, 8))
                t.transpose(o[:, 0:P], negc[:, :], ident).then_inc(S["cT"], 1)

            def s_(g):
                def f(b):
                    o = ring(f"s{g}", b)
                    if g == 0:
                        pe.wait_ge(S["Q3c"], nth("Q3c", b))
                        pe.wait_ge(S["Q3t"], nth("Q3t", b))
                        pe.wait_ge(S["KB"], nth("KB", b))
                        if is_first(b):
                            pe.wait_ge(S["sel"], 1)
                    t.matmul(o[:, :], KA[:, g, :], Q2[:, :, :].rearrange("p h n -> p (h n)"), start=True, stop=False)
                    t.matmul(o[:, :], KB[:, g, :], Q3[:, :, :].rearrange("p h n -> p (h n)"), start=False, stop=True).then_inc(S["s"], 1)
                return f

            def pv(n):
                def f(b):
                    if n > 0:
                        pe.wait_ge(S["vc"], nth("vc", b, n))
                    elif not is_first(b):
                        pe.wait_ge(S["vc"], nth("vc", b - 1, 2))
                    pe.wait_ge(S["pm"], nth("pm", b, NPT * n + NPT))
                    for k in range(NPT):
                        g = NPT * n + k
                        last = t.matmul(V_PS[32 * k:32 * k + 32, :], va[:, g * (HD + 1):g * (HD + 1) + 32],
                                        PT[:, slot(g), :, :].rearrange("p h n -> p (h n)"), start=True, stop=True)
                    last.then_inc(S["pv"], 1)
                return f

            def vt(n):
                def f(b):
                    o = ring(f"vt{n}", b)
                    pe.wait_ge(S["vc"], nth("vc", b, n + 1))
                    for h in range(HG):
                        last = t.transpose(o[:, h * P:(h + 1) * P], PT[:, n, h, :], ident)
                    last.then_inc(S["vt"], 1)
                return f

            def oT_(b):
                o = ring("oT", b)
                pe.wait_ge(S["on"], nth("on", b, 2))
                halves(o, o_nat).then_inc(S["oT2"], 1)

            def wo_(b):
                o = ring("wo", b)
                pe.wait_ge(S["oT2_sb"], nth("oT2_sb", b))
                product(o[:, 0:D], oT2, wo_sb).then_inc(S["wo"], 1)

            def xT(b):
                o = ring("xT", b)
                pe.wait_ge(S["x2n"], nth("x2n", b))
                halves(o, x2n).then_inc(S["xT"], 1)

            def three(o, hi, lo, whi, wlo, first, last_):
                t.matmul(o, hi, whi, start=first, stop=False)
                t.matmul(o, hi, wlo, start=False, stop=False)
                return t.matmul(o, lo, whi, start=False, stop=last_)

            def lg(b):
                o = ring("lg", b)
                if is_first(b):
                    pe.wait_ge(S["gate_lo"], 1)
                pe.wait_ge(S["xl"], nth("xl", b))
                for k in range(KC):
                    last = three(o[:, 0:NE], xh[:, k, :], xl[:, k, :], gate_hi[:, k, :], gate_lo[:, k, :], k == 0, k == KC - 1)
                last.then_inc(S["lg"], 1)

            def gu(j):
                def f(b):
                    if is_first(b):
                        pe.wait_ge(S["w_lo"], KC * (j + 1))
                    if j == 0:
                        pe.wait_ge(S["xl"], nth("xl", b))
                    if j > 0:
                        pe.wait_ge(S["av"], nth("av", b, j))
                    elif not is_first(b):
                        pe.wait_ge(S["av"], nth("av", b - 1, NJ))
                    for k in range(KC):
                        last = three(G_PS[:, 0:BW], xh[:, k, :], xl[:, k, :], wgu_hi[:, j, k, 0, :], wgu_lo[:, j, k, 0, :],
                                     k == 0, k == KC - 1)
                    last.then_inc(S["g"], 1)
                    if j > 0:
                        pe.wait_ge(S["bv"], nth("bv", b, j))
                    elif not is_first(b):
                        pe.wait_ge(S["bv"], nth("bv", b - 1, NJ))
                    for k in range(KC):
                        last = three(U_PS[:, 0:BW], xh[:, k, :], xl[:, k, :], wgu_hi[:, j, k, 1, :], wgu_lo[:, j, k, 1, :],
                                     k == 0, k == KC - 1)
                    last.then_inc(S["u"], 1)
                return f

            def T_(j):
                def f(b):
                    if j > 0:
                        pe.wait_ge(S["hl"], nth("hl", b, j))
                    elif not is_first(b):
                        pe.wait_ge(S["hl"], nth("hl", b - 1, NJ))
                    pe.wait_ge(S["h"], nth("h", b, j + 1))
                    for n in range(TC):
                        last = t.transpose(T_PS[:, n * P:(n + 1) * P], hv[:, n * P:(n + 1) * P], ident)
                    last.then_inc(S["T"], 1)
                return f

            def D_(j):
                def f(b):
                    if j == 0 and not is_first(b):
                        pe.wait_ge(S["y"], nth("y", b - 1))
                    if is_first(b):
                        pe.wait_ge(S["wd_lo"], j + 1)
                    pe.wait_ge(S["hl"], nth("hl", b, j + 1))
                    for n in range(TC):
                        last = three(Y_PS[:, 0:D], hh[:, n, :], hl[:, n, :], wd_hi[:, j, n, :], wd_lo[:, j, n, :],
                                     j == 0 and n == 0, j == NJ - 1 and n == TC - 1)
                    last.then_inc(S["dn"], 1)
                return f

            schedule(pe, {"r3": r3, "r4": r4, "r6": r6, "r7": r7, "r8": r8, "r9": r9, "r11": r11, "r12": r12, "r13": r13,
                          "r15": r15, "r16": r16, "r17": r17, "r18": r18, "r19": r19,
                          **{f"mx{u}": mx(u) for u in range(8)}, "c": c, **{f"s{g}": s_(g) for g in range(NG)},
                          **{f"pv{n}": pv(n) for n in range(2)}, **{f"vt{n}": vt(n) for n in range(2)}, "oT": oT_, "wo": wo_, "xT": xT, "lg": lg,
                          **{f"gu{j}": gu(j) for j in range(NJ)}, **{f"T{j}": T_(j) for j in range(NJ)},
                          **{f"D{j}": D_(j) for j in range(NJ)}})


def shape_constants(np):
    p = np.arange(P)
    c = np.zeros((P, CW), np.float32)
    c[:, 0:P] = np.eye(P)
    c[:, P:2 * P] = np.where(p[None, :] <= p[:, None], 0.0, -BIG)
    inv = (1.0 / np.float32(10000.0) ** (np.arange(0, DC, 2, dtype=np.float32) / np.float32(DC))).astype(np.float32)
    f = p.astype(np.float32)[:, None] * inv[None, :]
    cos, sin = np.concatenate([np.cos(f)] * 2, 1), np.concatenate([-np.sin(f), np.sin(f)], 1)
    scale = np.float32(1.0) / np.sqrt(np.float32(DC))
    at = 2 * P
    c[:, at:at + 2 * DC] = np.concatenate([cos * scale, cos], 1)
    c[:, at + 2 * DC:at + 4 * DC] = np.concatenate([sin * scale, sin], 1)
    at += 4 * DC
    c[:, at:at + NG] = (p[:, None] // HD) % NG == np.arange(NG)[None, :]
    c[:, at + NG:at + NG + HG] = p[:, None] % HG == np.arange(HG)[None, :]
    c[:, at + NG + HG:] = (p[:, None] % 32) // HG == np.arange(NG)[None, :]
    return c


def kernel(**inputs):
    import numpy as np
    import concourse.bacc as bacc
    from concourse import mybir as mb
    from concourse.bass_utils import run_bass_kernel_spmd as run

    a = {n: np.asarray(v) for n, v in inputs.items()}

    def cols(w):
        return w.T.reshape(KC, P, -1).transpose(1, 0, 2)

    wq, wkv = a["L0_attn_W_q_comp"].T, a["L0_attn_W_kv_comp"].T
    wk, wv = wkv[:, :DC], wkv[:, DC:]
    turn = np.concatenate([np.arange(DC // 2, DC), np.arange(DC // 2)])
    xq = a["L0_xattn_w_q"].reshape(NG, HG, HD, D).transpose(1, 0, 2, 3).reshape(D, D)
    arrays = {
        "x": a["x"],
        "ctxT": a["ctx_2048"].transpose(0, 2, 1).reshape(NB, KC, P, P).transpose(0, 2, 1, 3),
        "mask": a["mask_BxS2_if1"],
        "wgu": a["L0_ffn_gate_up_proj"].reshape(NJ, EJ, 2, NI, KC, P).transpose(5, 0, 4, 2, 1, 3).reshape(P, NJ, KC * 2 * BW),
        "wd": a["L0_ffn_down_proj"].transpose(0, 2, 1).reshape(NJ, TC, P, D).transpose(2, 0, 1, 3).reshape(P, NJ, TC * D),
        "gateT": cols(a["L0_ffn_gate_weight"]),
        "wtokv": a["L0_attn_W_to_kv"],
        "wcompT": a["L0_attn_W_compress"].T,
        "woutresT": a["L0_attn_W_out_res"].T,
        "wc2l": a["L0_attn_W_comp2lat"],
        "wqkv": np.concatenate([wq, wk, wq[:, turn], wk[:, turn], wv], 1),
        "gb": np.stack([a["L0_attn_ln_gamma"], a["L0_attn_ln_beta"]], 1),
        "bias2": np.broadcast_to(np.stack([a["L0_attn_b_out_res"], a["L0_xattn_b_o"]])[None], (P, 2, D)),
        "wq": cols(xq),
        "wkv": cols(np.concatenate([a["L0_xattn_w_k"], a["L0_xattn_w_v"]], 0)),
        "wo": cols(a["L0_xattn_w_o"]),
        "consts": shape_constants(np),
    }
    arrays = {n: np.ascontiguousarray(v) for n, v in arrays.items()}
    nc = bacc.Bacc("TRN2", target_bir_lowering=False, num_devices=1)
    args = {n: nc.dram_tensor(n + "_d", v.shape, mb.dt.from_np(v.dtype), kind="ExternalInput").ap() for n, v in arrays.items()}
    out = nc.dram_tensor("out_d", (NB, P, D), mb.dt.float32, kind="ExternalOutput").ap()
    decoder_kernel(nc, **args, out=out)
    r = run(nc, [{n + "_d": v for n, v in arrays.items()}], core_ids=[0])
    return r.results[0]["out_d"]
```
